# Optimizing a Trainium2 kernel written in Bass

```python
import numpy as np
import jax
import jax.numpy as jnp

def _softmax(x, axis=-1):
    return jax.nn.softmax(x, axis=axis)

def _gelu(x):
    return jax.nn.gelu(x, approximate=True)

def _silu(x):
    return jax.nn.silu(x)

def _sigmoid(x):
    return jax.nn.sigmoid(x)

def _layernorm(x, axis=-1, eps=1e-05):
    m = jnp.mean(x, axis=axis, keepdims=True)
    v = jnp.var(x, axis=axis, keepdims=True)
    return (x - m) / jnp.sqrt(v + eps)

def _scatter_add(tgt, idx, src, axis=0):
    return tgt.at[idx].add(src)

def _segment_sum(src, seg, n):
    return jax.ops.segment_sum(src, seg, n)
kernel_name = 'mk_vit_tower_postln_d2_tok_img768_r4_0d3096'

def setup_inputs(seed: int=0):
    np.random.seed(seed)
    _w = jnp.asarray

    def _rec_inputs():
        import jax
        import jax.numpy as jnp
        _rk = jax.random.key(seed)
        x = -0.00016672 + 0.999947 * jax.random.normal(jax.random.fold_in(_rk, 1), (64, 96, 96, 3), jnp.float32)
        return x
    x = _rec_inputs()

    def _L0_tok_setup():
        import jax, jax.numpy as jnp
        import numpy as np
        PATCH = 16

        def _patchify(images, p):
            B, H, W, C = images.shape
            gh, gw = (H // p, W // p)
            x = images.reshape(B, gh, p, gw, p, C)
            x = x.transpose(0, 1, 3, 2, 4, 5)
            return x.reshape(B, gh * gw, p * p * C)
        key = jax.random.key(seed)
        k1, k2, k3 = jax.random.split(key, 3)
        B, H, C, p, D = (64, 96, 3, PATCH, 192)
        N = (H // p) ** 2
        images = jax.random.normal(k1, (B, H, H, C), dtype=jnp.float32)
        W_proj = jax.random.normal(k2, (p * p * C, D), dtype=jnp.float32) * (1.0 / np.sqrt(p * p * C))
        b_proj = jnp.zeros((D,), dtype=jnp.float32)
        pos_table = jax.random.normal(k3, (N, D), dtype=jnp.float32) * 0.02
        return {'images': images, 'W_proj': W_proj, 'b_proj': b_proj, 'pos_table': pos_table}
    _L0_tok_all = _L0_tok_setup()
    _L0_tok_in = {k: v for k, v in _L0_tok_all.items() if k in ('W_proj', 'b_proj', 'pos_table')}
    del _L0_tok_all

    def _L0_attn_setup():
        import jax, jax.numpy as jnp
        import numpy as np
        import math
        D_MODEL, N_HEADS, D_HEAD, SEQ, BATCH = (192, 12, 64, 256, 8)
        INIT_RANGE = 0.02
        key = jax.random.key(seed)
        ks = jax.random.split(key, 6)
        x = jax.random.normal(ks[0], (BATCH, SEQ, D_MODEL), dtype=jnp.float32)
        W_Q = jax.random.normal(ks[1], (N_HEADS, D_MODEL, D_HEAD), dtype=jnp.float32) * INIT_RANGE
        W_K = jax.random.normal(ks[2], (N_HEADS, D_MODEL, D_HEAD), dtype=jnp.float32) * INIT_RANGE
        W_V = jax.random.normal(ks[3], (N_HEADS, D_MODEL, D_HEAD), dtype=jnp.float32) * INIT_RANGE
        W_O = jax.random.normal(ks[4], (N_HEADS, D_HEAD, D_MODEL), dtype=jnp.float32) * INIT_RANGE
        b_Q = jnp.zeros((N_HEADS, D_HEAD), dtype=jnp.float32)
        b_K = jnp.zeros((N_HEADS, D_HEAD), dtype=jnp.float32)
        b_V = jnp.zeros((N_HEADS, D_HEAD), dtype=jnp.float32)
        b_O = jnp.zeros((D_MODEL,), dtype=jnp.float32)
        return {'normalized_resid_pre': x, 'W_Q': W_Q, 'b_Q': b_Q, 'W_K': W_K, 'b_K': b_K, 'W_V': W_V, 'b_V': b_V, 'W_O': W_O, 'b_O': b_O}
    _L0_attn_all = _L0_attn_setup()
    _L0_attn_in = {k: v for k, v in _L0_attn_all.items() if k in ('W_Q', 'b_Q', 'W_K', 'b_K', 'W_V', 'b_V', 'W_O', 'b_O')}
    del _L0_attn_all

    def _L0_ffn_setup():
        import jax, jax.numpy as jnp
        import numpy as np
        H = 12
        ALPHA = (1, 2, 3)
        DEPTH = 5
        BLOCK_DEPTH = 3
        TOTAL_DEPTH_M1 = 14 - 1
        SMALL_ACTIVE = BLOCK_DEPTH <= DEPTH <= TOTAL_DEPTH_M1 - BLOCK_DEPTH

        def _ln(x, g, b, eps=1e-05):
            m = jnp.mean(x, axis=-1, keepdims=True)
            v = jnp.mean((x - m) ** 2, axis=-1, keepdims=True)
            return (x - m) * jax.lax.rsqrt(v + eps) * g + b

        def _attn_branch(xp, w_qkv, w_proj, b_proj, keep_heads, keep_ch):
            B2, N, C = xp.shape
            hd = C // H
            scale = hd ** (-0.5)
            qkv = (xp @ w_qkv).reshape(B2, N, 3, H, hd).transpose(2, 0, 3, 1, 4)
            hmask = (jnp.arange(H) < keep_heads).astype(xp.dtype)[None, :, None, None]
            q, k, v = (qkv[0] * hmask, qkv[1] * hmask, qkv[2] * hmask)
            a = jax.nn.softmax(jnp.einsum('bhnd,bhmd->bhnm', q, k) * scale, axis=-1)
            o = jnp.einsum('bhnm,bhmd->bhnd', a, v).transpose(0, 2, 1, 3).reshape(B2, N, C)
            o = o @ w_proj + b_proj
            cmask = (jnp.arange(C) < keep_ch).astype(xp.dtype)
            return o * cmask

        def _mlp_branch(xp, w1, b1, w2, b2, keep_ch):
            C = xp.shape[-1]
            cmask = (jnp.arange(C) < keep_ch).astype(xp.dtype)
            h = jax.nn.gelu(xp * cmask @ w1 + b1, approximate=False)
            return (h @ w2 + b2) * cmask
        key = jax.random.key(seed)
        ks = jax.random.split(key, 8)
        B, N, C = (64, 257, 192)
        HID = 4 * C

        def w(k, shape):
            return jax.random.normal(k, shape, jnp.float32) * 0.02
        return {'x': jax.random.normal(ks[0], (B, N, C), jnp.float32), 'gumbel_weights': jax.random.uniform(ks[1], (3,), jnp.float32), 'n1l_g': jnp.ones((C,), jnp.float32), 'n1l_b': jnp.zeros((C,), jnp.float32), 'n1s_g': jnp.ones((C,), jnp.float32), 'n1s_b': jnp.zeros((C,), jnp.float32), 'w_qkv': w(ks[2], (C, 3 * C)), 'w_proj': w(ks[3], (C, C)), 'b_proj': jnp.zeros((C,), jnp.float32), 'n2l_g': jnp.ones((C,), jnp.float32), 'n2l_b': jnp.zeros((C,), jnp.float32), 'n2s_g': jnp.ones((C,), jnp.float32), 'n2s_b': jnp.zeros((C,), jnp.float32), 'w_fc1': w(ks[4], (C, HID)), 'b_fc1': jnp.zeros((HID,), jnp.float32), 'w_fc2': w(ks[5], (HID, C)), 'b_fc2': jnp.zeros((C,), jnp.float32)}
    _L0_ffn_all = _L0_ffn_setup()
    _L0_ffn_in = {k: v for k, v in _L0_ffn_all.items() if k in ('gumbel_weights', 'n1l_g', 'n1l_b', 'n1s_g', 'n1s_b', 'w_qkv', 'w_proj', 'b_proj', 'n2l_g', 'n2l_b', 'n2s_g', 'n2s_b', 'w_fc1', 'b_fc1', 'w_fc2', 'b_fc2')}
    del _L0_ffn_all

    def _L1_attn_setup():
        import jax, jax.numpy as jnp
        import numpy as np
        H = 12

        def _alibi_bias(num_heads, n, dtype):
            ratio = 2.0 ** (-8.0 / num_heads)
            slopes = ratio ** jnp.arange(1, num_heads + 1, dtype=jnp.float32)
            pos = jnp.arange(n)
            rel = jnp.abs(pos[None, :] - pos[:, None]).astype(jnp.float32)
            return (-slopes[:, None, None] * rel[None]).astype(dtype)
        key = jax.random.key(seed)
        ks = jax.random.split(key, 5)
        B, N, C = (16, 256, 192)
        s = 0.02
        return {'x': jax.random.normal(ks[0], (B, N, C), jnp.float32), 'w_qkv': jax.random.normal(ks[1], (3 * C, C), jnp.float32) * s, 'b_qkv': jax.random.normal(ks[2], (3 * C,), jnp.float32) * s, 'w_proj': jax.random.normal(ks[3], (C, C), jnp.float32) * s, 'b_proj': jax.random.normal(ks[4], (C,), jnp.float32) * s}
    _L1_attn_all = _L1_attn_setup()
    _L1_attn_in = {k: v for k, v in _L1_attn_all.items() if k in ('w_qkv', 'b_qkv', 'w_proj', 'b_proj')}
    del _L1_attn_all

    def _L1_ffn_setup():
        import jax, jax.numpy as jnp
        import numpy as np
        B, S, D = (4, 256, 192)
        E = 8
        H = 192
        HS = 768
        TOPK_ROUTED = 2
        key = jax.random.key(seed)
        ks = jax.random.split(key, 10)
        w = lambda k, shape: jax.random.normal(k, shape, dtype=jnp.float32) * 0.02
        return {'x': jax.random.normal(ks[0], (B, S, D), dtype=jnp.float32), 'router_w': w(ks[1], (D, E)), 'w_gate': w(ks[2], (E, D, H)), 'w_up': w(ks[3], (E, D, H)), 'w_down': w(ks[4], (E, H, D)), 'ws_gate': w(ks[5], (D, HS)), 'ws_up': w(ks[6], (D, HS)), 'ws_down': w(ks[7], (HS, D)), 'sg_w': w(ks[8], (D, 1)), 'sg_b': jnp.zeros((1,), jnp.float32)}
    _L1_ffn_all = _L1_ffn_setup()
    _L1_ffn_in = {k: v for k, v in _L1_ffn_all.items() if k in ('router_w', 'w_gate', 'w_up', 'w_down', 'ws_gate', 'ws_up', 'ws_down', 'sg_w', 'sg_b')}
    del _L1_ffn_all
    return {'x': x, 'L0_tok_W_proj': _L0_tok_in['W_proj'], 'L0_tok_b_proj': _L0_tok_in['b_proj'], 'L0_tok_pos_table': _L0_tok_in['pos_table'], 'L0_attn_W_Q': _L0_attn_in['W_Q'], 'L0_attn_b_Q': _L0_attn_in['b_Q'], 'L0_attn_W_K': _L0_attn_in['W_K'], 'L0_attn_b_K': _L0_attn_in['b_K'], 'L0_attn_W_V': _L0_attn_in['W_V'], 'L0_attn_b_V': _L0_attn_in['b_V'], 'L0_attn_W_O': _L0_attn_in['W_O'], 'L0_attn_b_O': _L0_attn_in['b_O'], 'L0_ffn_gumbel_weights': _L0_ffn_in['gumbel_weights'], 'L0_ffn_n1l_g': _L0_ffn_in['n1l_g'], 'L0_ffn_n1l_b': _L0_ffn_in['n1l_b'], 'L0_ffn_n1s_g': _L0_ffn_in['n1s_g'], 'L0_ffn_n1s_b': _L0_ffn_in['n1s_b'], 'L0_ffn_w_qkv': _L0_ffn_in['w_qkv'], 'L0_ffn_w_proj': _L0_ffn_in['w_proj'], 'L0_ffn_b_proj': _L0_ffn_in['b_proj'], 'L0_ffn_n2l_g': _L0_ffn_in['n2l_g'], 'L0_ffn_n2l_b': _L0_ffn_in['n2l_b'], 'L0_ffn_n2s_g': _L0_ffn_in['n2s_g'], 'L0_ffn_n2s_b': _L0_ffn_in['n2s_b'], 'L0_ffn_w_fc1': _L0_ffn_in['w_fc1'], 'L0_ffn_b_fc1': _L0_ffn_in['b_fc1'], 'L0_ffn_w_fc2': _L0_ffn_in['w_fc2'], 'L0_ffn_b_fc2': _L0_ffn_in['b_fc2'], 'L1_attn_w_qkv': _L1_attn_in['w_qkv'], 'L1_attn_b_qkv': _L1_attn_in['b_qkv'], 'L1_attn_w_proj': _L1_attn_in['w_proj'], 'L1_attn_b_proj': _L1_attn_in['b_proj'], 'L1_ffn_router_w': _L1_ffn_in['router_w'], 'L1_ffn_w_gate': _L1_ffn_in['w_gate'], 'L1_ffn_w_up': _L1_ffn_in['w_up'], 'L1_ffn_w_down': _L1_ffn_in['w_down'], 'L1_ffn_ws_gate': _L1_ffn_in['ws_gate'], 'L1_ffn_ws_up': _L1_ffn_in['ws_up'], 'L1_ffn_ws_down': _L1_ffn_in['ws_down'], 'L1_ffn_sg_w': _L1_ffn_in['sg_w'], 'L1_ffn_sg_b': _L1_ffn_in['sg_b']}

def reference(x, L0_tok_W_proj, L0_tok_b_proj, L0_tok_pos_table, L0_attn_W_Q, L0_attn_b_Q, L0_attn_W_K, L0_attn_b_K, L0_attn_W_V, L0_attn_b_V, L0_attn_W_O, L0_attn_b_O, L0_ffn_gumbel_weights, L0_ffn_n1l_g, L0_ffn_n1l_b, L0_ffn_n1s_g, L0_ffn_n1s_b, L0_ffn_w_qkv, L0_ffn_w_proj, L0_ffn_b_proj, L0_ffn_n2l_g, L0_ffn_n2l_b, L0_ffn_n2s_g, L0_ffn_n2s_b, L0_ffn_w_fc1, L0_ffn_b_fc1, L0_ffn_w_fc2, L0_ffn_b_fc2, L1_attn_w_qkv, L1_attn_b_qkv, L1_attn_w_proj, L1_attn_b_proj, L1_ffn_router_w, L1_ffn_w_gate, L1_ffn_w_up, L1_ffn_w_down, L1_ffn_ws_gate, L1_ffn_ws_up, L1_ffn_ws_down, L1_ffn_sg_w, L1_ffn_sg_b):
    import jax
    import jax.numpy as jnp

    def _L0_tok_ref(images, W_proj, b_proj, pos_table):
        import jax, jax.numpy as jnp
        import numpy as np
        PATCH = 16

        def _patchify(images, p):
            B, H, W, C = images.shape
            gh, gw = (H // p, W // p)
            x = images.reshape(B, gh, p, gw, p, C)
            x = x.transpose(0, 1, 3, 2, 4, 5)
            return x.reshape(B, gh * gw, p * p * C)
        patches = _patchify(images, PATCH)
        emb = jnp.einsum('bnk,kd->bnd', patches, W_proj) + b_proj
        return emb + pos_table[None, :, :]

    def _L0_attn_ref(normalized_resid_pre, W_Q, b_Q, W_K, b_K, W_V, b_V, W_O, b_O):
        import jax, jax.numpy as jnp
        import numpy as np
        import math
        D_MODEL, N_HEADS, D_HEAD, SEQ, BATCH = (192, 12, 64, 256, 8)
        INIT_RANGE = 0.02
        x = normalized_resid_pre
        q = jnp.einsum('bsd,hde->bshe', x, W_Q) + b_Q
        k = jnp.einsum('bsd,hde->bshe', x, W_K) + b_K
        v = jnp.einsum('bsd,hde->bshe', x, W_V) + b_V
        scores = jnp.einsum('bqhe,bkhe->bhqk', q, k) / math.sqrt(D_HEAD)
        s = x.shape[1]
        causal = jnp.tril(jnp.ones((s, s), dtype=bool))
        scores = jnp.where(causal[None, None], scores, -jnp.inf)
        pattern = jax.nn.softmax(scores, axis=-1)
        pattern = jnp.where(jnp.isnan(pattern), 0.0, pattern)
        z = jnp.einsum('bhqk,bkhe->bqhe', pattern, v)
        attn_out = jnp.einsum('bqhe,hed->bqd', z, W_O) + b_O
        return attn_out

    def _L0_ffn_ref(x, gumbel_weights, n1l_g, n1l_b, n1s_g, n1s_b, w_qkv, w_proj, b_proj, n2l_g, n2l_b, n2s_g, n2s_b, w_fc1, b_fc1, w_fc2, b_fc2):
        import jax, jax.numpy as jnp
        import numpy as np
        H = 12
        ALPHA = (1, 2, 3)
        DEPTH = 5
        BLOCK_DEPTH = 3
        TOTAL_DEPTH_M1 = 14 - 1
        SMALL_ACTIVE = BLOCK_DEPTH <= DEPTH <= TOTAL_DEPTH_M1 - BLOCK_DEPTH

        def _ln(x, g, b, eps=1e-05):
            m = jnp.mean(x, axis=-1, keepdims=True)
            v = jnp.mean((x - m) ** 2, axis=-1, keepdims=True)
            return (x - m) * jax.lax.rsqrt(v + eps) * g + b

        def _attn_branch(xp, w_qkv, w_proj, b_proj, keep_heads, keep_ch):
            B2, N, C = xp.shape
            hd = C // H
            scale = hd ** (-0.5)
            qkv = (xp @ w_qkv).reshape(B2, N, 3, H, hd).transpose(2, 0, 3, 1, 4)
            hmask = (jnp.arange(H) < keep_heads).astype(xp.dtype)[None, :, None, None]
            q, k, v = (qkv[0] * hmask, qkv[1] * hmask, qkv[2] * hmask)
            a = jax.nn.softmax(jnp.einsum('bhnd,bhmd->bhnm', q, k) * scale, axis=-1)
            o = jnp.einsum('bhnm,bhmd->bhnd', a, v).transpose(0, 2, 1, 3).reshape(B2, N, C)
            o = o @ w_proj + b_proj
            cmask = (jnp.arange(C) < keep_ch).astype(xp.dtype)
            return o * cmask

        def _mlp_branch(xp, w1, b1, w2, b2, keep_ch):
            C = xp.shape[-1]
            cmask = (jnp.arange(C) < keep_ch).astype(xp.dtype)
            h = jax.nn.gelu(xp * cmask @ w1 + b1, approximate=False)
            return (h @ w2 + b2) * cmask
        B, N, C = x.shape
        B2 = B // 2
        nl = _ln(x[:B2], n1l_g, n1l_b)
        ns = _ln(x[B2:], n1s_g, n1s_b)
        a_large = _attn_branch(nl, w_qkv, w_proj, b_proj, H, C)
        if SMALL_ACTIVE:
            a_small = sum((gumbel_weights[i] * _attn_branch(ns, w_qkv, w_proj, b_proj, H // ALPHA[i], C // ALPHA[i]) for i in range(3)))
            attn_out = jnp.concatenate([a_large, a_small], axis=0)
        else:
            attn_out = jnp.concatenate([a_large, a_large], axis=0)
        x = x + attn_out
        nl2 = _ln(x[:B2], n2l_g, n2l_b)
        ns2 = _ln(x[B2:], n2s_g, n2s_b)
        m_large = _mlp_branch(nl2, w_fc1, b_fc1, w_fc2, b_fc2, C)
        if SMALL_ACTIVE:
            m_small = sum((gumbel_weights[i] * _mlp_branch(ns2, w_fc1, b_fc1, w_fc2, b_fc2, C // ALPHA[i]) for i in range(3)))
            mlp_out = jnp.concatenate([m_large, m_small], axis=0)
        else:
            mlp_out = jnp.concatenate([m_large, m_large], axis=0)
        return x + mlp_out

    def _L1_attn_ref(x, w_qkv, b_qkv, w_proj, b_proj):
        import jax, jax.numpy as jnp
        import numpy as np
        H = 12

        def _alibi_bias(num_heads, n, dtype):
            ratio = 2.0 ** (-8.0 / num_heads)
            slopes = ratio ** jnp.arange(1, num_heads + 1, dtype=jnp.float32)
            pos = jnp.arange(n)
            rel = jnp.abs(pos[None, :] - pos[:, None]).astype(jnp.float32)
            return (-slopes[:, None, None] * rel[None]).astype(dtype)
        B, N, C = x.shape
        D = C // H
        scale = D ** (-0.5)
        qkv = x @ w_qkv.T + b_qkv
        qkv = qkv.reshape(B, N, 3, H, D)
        q = qkv[:, :, 0].transpose(0, 2, 1, 3)
        k = qkv[:, :, 1].transpose(0, 2, 1, 3)
        v = qkv[:, :, 2].transpose(0, 2, 1, 3)
        bias = _alibi_bias(H, N, x.dtype)
        scores = jnp.einsum('bhnd,bhmd->bhnm', q, k) * scale + bias[None]
        attn = jax.nn.softmax(scores, axis=-1)
        out = jnp.einsum('bhnm,bhmd->bhnd', attn, v)
        out = out.transpose(0, 2, 1, 3).reshape(B, N, C)
        return out @ w_proj.T + b_proj

    def _L1_ffn_ref(x, router_w, w_gate, w_up, w_down, ws_gate, ws_up, ws_down, sg_w, sg_b):
        import jax, jax.numpy as jnp
        import numpy as np
        B, S, D = (4, 256, 192)
        E = 8
        H = 192
        HS = 768
        TOPK_ROUTED = 2
        probs = jax.nn.softmax(x @ router_w, axis=-1)
        gates, idx = jax.lax.top_k(probs, TOPK_ROUTED)
        gates = gates / jnp.sum(gates, axis=-1, keepdims=True)
        n_exp = router_w.shape[1]
        dense_g = jnp.sum(jax.nn.one_hot(idx, n_exp, dtype=x.dtype) * gates[..., None], axis=-2)
        g = jax.nn.silu(jnp.einsum('bsd,edh->bseh', x, w_gate))
        u = jnp.einsum('bsd,edh->bseh', x, w_up)
        expert_out = jnp.einsum('bseh,ehd->bsed', g * u, w_down)
        routed = jnp.einsum('bse,bsed->bsd', dense_g, expert_out)
        shared = jax.nn.silu(x @ ws_gate) * (x @ ws_up) @ ws_down
        alpha = jax.nn.sigmoid(x @ sg_w + sg_b)
        return alpha * shared + (1.0 - alpha) * routed
    h = _L0_tok_ref(x, L0_tok_W_proj, L0_tok_b_proj, L0_tok_pos_table)
    h = _layernorm(h + _L0_attn_ref(h, L0_attn_W_Q, L0_attn_b_Q, L0_attn_W_K, L0_attn_b_K, L0_attn_W_V, L0_attn_b_V, L0_attn_W_O, L0_attn_b_O), axis=-1)
    h = _layernorm(h + _L0_ffn_ref(h, L0_ffn_gumbel_weights, L0_ffn_n1l_g, L0_ffn_n1l_b, L0_ffn_n1s_g, L0_ffn_n1s_b, L0_ffn_w_qkv, L0_ffn_w_proj, L0_ffn_b_proj, L0_ffn_n2l_g, L0_ffn_n2l_b, L0_ffn_n2s_g, L0_ffn_n2s_b, L0_ffn_w_fc1, L0_ffn_b_fc1, L0_ffn_w_fc2, L0_ffn_b_fc2), axis=-1)
    h = _layernorm(h + _L1_attn_ref(h, L1_attn_w_qkv, L1_attn_b_qkv, L1_attn_w_proj, L1_attn_b_proj), axis=-1)
    h = _layernorm(h + _L1_ffn_ref(h, L1_ffn_router_w, L1_ffn_w_gate, L1_ffn_w_up, L1_ffn_w_down, L1_ffn_ws_gate, L1_ffn_ws_up, L1_ffn_ws_down, L1_ffn_sg_w, L1_ffn_sg_b), axis=-1)
    return h

_drawn_inputs = setup_inputs


def setup_inputs(seed=0):
    import zlib

    import numpy as np

    out = dict(_drawn_inputs(seed))
    spreads = {'L0_tok_b_proj': (0.0, 0.1),
     'L0_attn_b_Q': (0.0, 0.8),
     'L0_attn_b_K': (0.0, 2.0),
     'L0_attn_b_V': (0.0, 0.1),
     'L0_attn_b_O': (0.0, 0.1),
     'L0_ffn_n1l_g': (1.0, 0.6),
     'L0_ffn_n1l_b': (0.0, 0.8),
     'L0_ffn_n1s_g': (1.0, 0.6),
     'L0_ffn_n1s_b': (0.0, 0.8),
     'L0_ffn_b_proj': (0.0, 0.1),
     'L0_ffn_n2l_g': (1.0, 0.6),
     'L0_ffn_n2l_b': (0.0, 2.0),
     'L0_ffn_n2s_g': (1.0, 0.6),
     'L0_ffn_n2s_b': (0.0, 2.0),
     'L0_ffn_b_fc1': (0.0, 0.755),
     'L0_ffn_b_fc2': (0.0, 0.1)}
    factors = {'L0_tok_pos_table': 2.829,
     'L0_attn_W_Q': 8.0,
     'L0_attn_W_K': 8.0,
     'L0_ffn_gumbel_weights': 6.234,
     'L0_ffn_w_qkv': 7.423,
     'L0_ffn_w_proj': 8.0,
     'L1_attn_b_qkv': 8.0,
     'L1_attn_b_proj': 2.94,
     'L1_ffn_router_w': 8.0,
     'L1_ffn_w_gate': 8.0,
     'L1_ffn_w_up': 8.0,
     'L1_ffn_w_down': 8.0,
     'L1_ffn_ws_gate': 5.149,
     'L1_ffn_ws_up': 5.1,
     'L1_ffn_ws_down': 5.089,
     'L1_ffn_sg_w': 8.0}
    for name, (base, spread) in spreads.items():
        noise = np.random.default_rng([zlib.crc32(name.encode()), seed]).standard_normal(out[name].shape)
        drawn = base * np.exp(spread * noise) if base else spread * noise
        out[name] = jnp.asarray(drawn.astype(out[name].dtype))
    for name, factor in factors.items():
        out[name] = (out[name] * factor).astype(out[name].dtype)
    return out
```

```python
from contextlib import ExitStack

import numpy as np

import concourse.bass as bass
import concourse.mybir as mybir

F32 = mybir.dt.float32
F32R = mybir.dt.float32r
U32 = mybir.dt.uint32
ALU = mybir.AluOpType
ACT = mybir.ActivationFunctionType
AX = mybir.AxisListType

P = 128
IMAGES, SIDE, PATCH = 64, 96, 16
SEQ = (SIDE // PATCH) ** 2
TOK = IMAGES * SEQ
D = 192
DB = D - P
PATCH_K = PATCH * PATCH * 3
HEADS = 12
HID = 768
EXPERTS = 8
EH = EXPERTS * D
EPS = 1e-5
NEG = -1e30

UNIT = 2 * SEQ
UNITS = 4
TILE = 96
TILES = 3
WIDE = UNITS * UNIT
HB = HEADS // 2
MT = 128
MW = 3 * MT
BANK = 512


class Split:

    def __init__(self, sb, name, n):
        self.n = n
        self.a_hi = sb(name + "_a_hi", [P, n], F32R)
        self.a_lo = sb(name + "_a_lo", [P, n], F32R)
        self.b_hi = sb(name + "_b_hi", [P, n], F32R)
        self.b_lo = sb(name + "_b_lo", [DB, n], F32R)


class SplitX:

    def __init__(self, sb, name, n):
        self.a_hi = sb(name + "_a_hi", [P, n], F32R)
        self.a_lo = sb(name + "_a_lo", [P, n], F32R)
        self.b = sb(name + "_b", [P, n], F32R)


def weight_by_x(nc, out, w, cols, x, toks):
    nc.tensor.matmul(out, w.a_hi[:, cols], x.a_hi[:, toks], start=True, stop=False)
    nc.tensor.matmul(out, w.a_hi[:, cols], x.a_lo[:, toks], start=False, stop=False)
    nc.tensor.matmul(out, w.a_lo[:, cols], x.a_hi[:, toks], start=False, stop=False)
    nc.tensor.matmul(out, w.b_hi[:, cols], x.b[:, toks], start=False, stop=False)
    return nc.tensor.matmul(out, w.b_lo[:, cols], x.b[0:DB, toks], start=False, stop=True)


def weight_by_x_head(nc, out, w, cols, x, toks, k):
    nc.tensor.matmul(out, w.a_hi[0:k, cols], x.a_hi[0:k, toks], start=True, stop=False)
    nc.tensor.matmul(out, w.a_hi[0:k, cols], x.a_lo[0:k, toks], start=False, stop=False)
    return nc.tensor.matmul(out, w.a_lo[0:k, cols], x.a_hi[0:k, toks], start=False, stop=True)


def x_by_weight(nc, out, x, toks, w, cols):
    nc.tensor.matmul(out, x.a_hi[:, toks], w.a_hi[:, cols], start=True, stop=False)
    nc.tensor.matmul(out, x.a_lo[:, toks], w.a_hi[:, cols], start=False, stop=False)
    nc.tensor.matmul(out, x.a_hi[:, toks], w.a_lo[:, cols], start=False, stop=False)
    nc.tensor.matmul(out, x.b[:, toks], w.b_hi[:, cols], start=False, stop=False)
    return nc.tensor.matmul(out, x.b[0:DB, toks], w.b_lo[:, cols], start=False, stop=True)


def column(v):
    return v.rearrange("(p a) -> p a", a=1)


def rows(v, p):
    return v.rearrange("(a n) -> a n", a=1).to_broadcast([p, v.shape[0]])


def wait_apart(eng, sem, value):
    eng.wait_ge(sem, value)
    eng.nop(nofuse=True)


class Sems:

    def __init__(self, nc, prefix):
        self._nc, self._prefix, self._made = nc, prefix, {}

    def __enter__(self):
        return self

    def __exit__(self, *_):
        self._nc.clear_and_free_semaphores(list(self._made.values()))
        self._nc.all_engine_barrier()

    def __getitem__(self, name):
        if name not in self._made:
            self._made[name] = self._nc.alloc_semaphore(name=f"{self._prefix}_{name}")
        return self._made[name]



def slot_heads(hb_rows):
    per_chunk = P // hb_rows
    half = max(1, per_chunk // 2)
    order = []
    for b in range(2):
        for j in range(b * half, (b + 1) * half):
            order += [c * per_chunk + j for c in range(HEADS // per_chunk)]
    return order


def attention_stage(nc, psum, ident, neg_half, name, src, dst, n_iter, dh, hb_rows, w_q, w_k, w_v, w_o,
                    bias_hk, q_bias, k_bias, q_scale, out_bias, prenorm, postnorm, side=None):
    heads_per_chunk = P // hb_rows
    chunks = HEADS // heads_per_chunk
    z_banks = 2 if dh == 64 else 1
    zh = HEADS // z_banks
    z_chunks = [(c * P, min(P, HEADS * dh - c * P)) for c in range(-(-HEADS * dh // P))]
    v_cols = HEADS * dh // z_banks
    slots = slot_heads(hb_rows)
    tile_heads = HEADS // heads_per_chunk

    with Sems(nc, name) as S, ExitStack() as ctx:
        def sb(nm, shape, dt=F32):
            return ctx.enter_context(nc.sbuf_tensor(f"{name}_{nm}", shape, dt))

        x_tok = sb("x_tok", [TILE, TILES, D])
        residual = sb("residual", [TILE, TILES, D])
        y = sb("y", [TILE, TILES, D])
        xs = SplitX(sb, "x", WIDE)
        q = [sb(f"q{c}", [P, WIDE]) for c in range(chunks)]
        k = [sb(f"k{c}", [P, WIDE]) for c in range(chunks)]
        v = [sb(f"v{p}", [UNIT, HEADS, dh + 1]) for p in range(2)]
        prob = [sb(f"prob{p}", [UNIT, HEADS, UNIT]) for p in range(2)]
        row_max = [sb(f"row_max{p}", [UNIT, HEADS]) for p in range(2)]
        prob_t = sb("prob_t", [UNIT, HEADS, UNIT])
        z_recip = sb("z_recip", [UNIT, HEADS])
        z = sb("z", [UNIT, HEADS, dh])
        z_t = sb("z_t", [P, len(z_chunks), WIDE])
        stats = sb("stats", [TILE, TILES, 6])
        mean_var = sb("mean_var", [TILE, TILES, 2])
        var_eps = sb("var_eps", [TILE, TILES])
        rstd = sb("rstd", [TILE, TILES])
        if prenorm:
            x_hat = sb("x_hat", [TILE, TILES, D])
            x_aff_a, x_aff_b = sb("x_aff_a", [P, WIDE]), sb("x_aff_b", [DB, WIDE])
            pre_stats = sb("pre_stats", [TILE, TILES, 6])
            pre_mv = sb("pre_mv", [TILE, TILES, 2])
            pre_var = sb("pre_var", [TILE, TILES])
            pre_rstd = sb("pre_rstd", [TILE, TILES])

        def bank(b):
            return psum[:, b * BANK:(b + 1) * BANK]

        def scores_bank(b, p=UNIT):
            return bank(b)[0:p, 0:HB * UNIT].rearrange("p (h k) -> p h k", h=HB)

        z_ps = psum[:, 6 * BANK:8 * BANK].rearrange("p (b n) -> p b n", b=2)[
            0:UNIT, 0:z_banks, 0:zh * (dh + 1)].rearrange("p b (h e) -> p b h e", e=dh + 1)
        zt_ps = bank(5)[:, 0:len(z_chunks) * UNIT].rearrange("p (c t) -> p c t", t=UNIT)

        block = ctx.enter_context(nc.Block())

        @block.sync
        def _(sp):
            def load(i):
                sp.wait_ge(S["residual_ready"], i)
                sp.wait_ge(S["x_hat_ready" if prenorm else "x_transposed"], i)
                sp.dma_start(x_tok[:, :, :], src(i)).then_inc(S["x_loaded"], 16)

            def store(i):
                sp.wait_ge(S["y_ready" if postnorm else "attn_added"], TILES * i + TILES)
                sp.dma_start(dst(i), y[:, :, :]).then_inc(S["y_stored"], 16)

            sp.dma_start(x_tok[:, :, :], src(0)).then_inc(S["x_loaded"], 16)
            if side:
                side.load_start(sp)
            with sp.Fori(0, n_iter - 1) as i:
                load(i + 1)
                if side:
                    side.load_step(sp, i)
                store(i)
            if side:
                side.load_step(sp, n_iter - 1)
            store(n_iter - 1)
            sp.wait_ge(S["y_stored"], 16 * n_iter)

        @block.gpsimd
        def _(pool):
            for p in range(2):
                nc.gpsimd.memset(v[p][:, :, dh:dh + 1], 1.0).then_inc(S["ones_set"], 1)

            def pre(i):
                pool.wait_ge(S["x_loaded"], 16 * i + 16)
                pool.wait_ge(S["attn_added"], TILES * i)
                nc.gpsimd.tensor_tensor(residual[:, :, :], x_tok[:, :, :],
                                        out_bias.rearrange("p (a n) -> p a n", a=1)
                                        .to_broadcast([TILE, TILES, D]), ALU.add
                                        ).then_inc(S["residual_ready"], 1)

            def pre_pow(i):
                pool.wait_ge(S["pre_var_ready"], i + 1)
                nc.gpsimd.tensor_tensor(pre_rstd[:, :], pre_var[:, :],
                                        neg_half[0:TILE, 0:TILES], ALU.pow
                                        ).then_inc(S["pre_rstd_ready"], 1)

            def out_pow(i, t):
                pool.wait_ge(S["var_ready"], TILES * i + t + 1)
                nc.gpsimd.tensor_tensor(rstd[:, t:t + 1], var_eps[:, t:t + 1],
                                        neg_half[0:TILE, 0:1], ALU.pow).then_inc(S["rstd_ready"], 1)

            if prenorm:
                pre_pow(0)
            if side:
                side.split_start(pool)

            def body(i, last):
                pre(i)
                if prenorm and not last:
                    pre_pow(i + 1)
                if side:
                    side.split_step(pool, i)
                if postnorm:
                    for t in range(TILES):
                        out_pow(i, t)

            with pool.Fori(0, n_iter - 1) as i:
                body(i, False)
            body(n_iter - 1, True)

        @block.tensor
        def _(pe):
            def transpose_x(i):
                pe.wait_ge(S["x_loaded"], 16 * i + 16)
                if prenorm:
                    pe.wait_ge(S["x_hat_ready"], i + 1)
                pe.wait_ge(S["v_evacuated"], UNITS * i)
                tok = x_hat if prenorm else x_tok
                for t in range(TILES):
                    nc.tensor.transpose(bank(0)[:, t * TILE:(t + 1) * TILE], tok[:, t, 0:P],
                                        ident[0:TILE, 0:TILE])
                    last = nc.tensor.transpose(bank(1)[0:DB, t * TILE:(t + 1) * TILE], tok[:, t, P:D],
                                               ident[0:TILE, 0:TILE])
                last.then_inc(S["x_transposed"], 1)

            def project_qk(i, c0, c1):
                for c in range(c0, c1):
                    if c == 0:
                        pe.wait_ge(S["x_split"], i + 1)
                    elif c >= 2:
                        pe.wait_ge(S["qk_evacuated"], 2 * chunks * i + c - 1)
                    w = w_q if c < chunks else w_k
                    at = (c % chunks) * P
                    weight_by_x(nc, bank(c % 2)[:, 0:WIDE], w, slice(at, at + P), xs, slice(0, WIDE)
                                ).then_inc(S["qk_done"], 1)

            def scores(i, s):
                if s == 0:
                    pe.wait_ge(S["qk_evacuated"], 2 * chunks * (i + 1))
                pe.wait_ge(S["scores_biased"], 2 * (UNITS * i + s))
                toks = slice(s * UNIT, (s + 1) * UNIT)
                for part in range(HB // tile_heads):
                    for b in range(2):
                        if part > 0:
                            pe.wait_ge(S["scores_part"], 2 * (UNITS * i + s) + b + 1)
                        for hh in range(part * tile_heads, (part + 1) * tile_heads):
                            h = slots[b * HB + hh]
                            c, r = h // heads_per_chunk, (h % heads_per_chunk) * hb_rows
                            last = nc.tensor.matmul(scores_bank(2 + b)[:, hh, :],
                                                    q[c][r:r + hb_rows, toks],
                                                    k[c][r:r + hb_rows, toks], start=True, stop=True)
                        done = part == HB // tile_heads - 1
                        last.then_inc(S["scores_done" if done else "scores_part"], 1)

            def values(i, s):
                pe.wait_ge(S["v_evacuated"], UNITS * i + s)
                toks = slice(s * UNIT, (s + 1) * UNIT)
                for b in range(z_banks):
                    last = x_by_weight(nc, bank(b)[0:UNIT, 0:v_cols], xs, toks, w_v,
                                       slice(b * v_cols, (b + 1) * v_cols))
                last.then_inc(S["v_done"], 1)

            def transpose_prob(i, s):
                if s == 0:
                    pe.wait_ge(S["attn_added"], TILES * i)
                elif s == 3:
                    pe.wait_ge(S["attn_added"], TILES * i + 1)
                for b in range(2):
                    if b == 1:
                        pe.wait_ge(S["zt_evacuated"], UNITS * i + s)
                    pe.wait_ge(S["exp_done"], 2 * (UNITS * i + s) + b + 1)
                    for hh in range(HB):
                        last = nc.tensor.transpose(scores_bank(4 + b)[:, hh, :],
                                                   prob[s % 2][:, b * HB + hh, :],
                                                   ident[0:UNIT, 0:UNIT])
                    last.then_inc(S["prob_transposed"], 1)

            def mix_values(i, s):
                pe.wait_ge(S["v_evacuated"], UNITS * i + s + 1)
                pe.wait_ge(S["ones_set"], 2)
                pe.wait_ge(S["z_normalised"], UNITS * i + s)
                for n, h in enumerate(slots):
                    if n % HB == 0:
                        pe.wait_ge(S["prob_t_evacuated"], 2 * (UNITS * i + s) + n // HB + 1)
                    last = nc.tensor.matmul(z_ps[:, h // zh, h % zh, :], prob_t[:, n, :],
                                            v[s % 2][:, h, :], start=True, stop=True)
                last.then_inc(S["values_mixed"], 1)

            def transpose_z(i, s):
                pe.wait_ge(S["z_normalised"], UNITS * i + s + 1)
                flat = z[:, :, :].rearrange("p h e -> p (h e)")
                for n, (at, m) in enumerate(z_chunks):
                    last = nc.tensor.transpose(zt_ps[0:m, n, :], flat[:, at:at + m],
                                               ident[0:UNIT, 0:UNIT])
                last.then_inc(S["z_transposed"], 1)

            def project_out(i, t):
                pe.wait_ge(S["zt_evacuated"], UNITS * i + t + 2)
                if t == 2:
                    pe.wait_ge(S["attn_added"], TILES * i + 2)
                out = bank(4)[0:TILE, 0:D]
                for n, (_, m) in enumerate(z_chunks):
                    last = nc.tensor.matmul(out, z_t[0:m, n, t * TILE:(t + 1) * TILE], w_o[0:m, n, :],
                                            start=(n == 0), stop=(n == len(z_chunks) - 1))
                last.then_inc(S["out_done"], 1)

            def body(i, last):
                scores(i, 0)
                values(i, 0)
                scores(i, 1)
                values(i, 1)
                transpose_prob(i, 0)
                mix_values(i, 0)
                scores(i, 2)
                values(i, 2)
                transpose_z(i, 0)
                transpose_prob(i, 1)
                mix_values(i, 1)
                scores(i, 3)
                values(i, 3)
                if not last:
                    transpose_x(i + 1)
                transpose_z(i, 1)
                transpose_prob(i, 2)
                mix_values(i, 2)
                project_out(i, 0)
                if not last:
                    project_qk(i + 1, 0, chunks)
                transpose_z(i, 2)
                transpose_prob(i, 3)
                mix_values(i, 3)
                project_out(i, 1)
                if not last:
                    project_qk(i + 1, chunks, 2 * chunks)
                transpose_z(i, 3)
                project_out(i, 2)

            transpose_x(0)
            project_qk(0, 0, 2 * chunks)
            with pe.Fori(0, n_iter - 1) as i:
                body(i, False)
            body(n_iter - 1, True)

        @block.scalar
        def _(act):
            def round_x(i):
                act.wait_ge(S["x_transposed"], i + 1)
                if prenorm:
                    ga, gb, ba, bb = prenorm
                    nc.scalar.activation(xs.a_hi[:, :], bank(0)[:, 0:WIDE], ACT.Identity, bias=ba, scale=ga
                                         ).then_inc(S["x_rounded"], 1)
                    nc.scalar.activation(xs.b[0:DB, :], bank(1)[0:DB, 0:WIDE], ACT.Identity, bias=bb,
                                         scale=gb).then_inc(S["x_rounded"], 1)
                else:
                    nc.scalar.activation(xs.a_hi[:, :], bank(0)[:, 0:WIDE], ACT.Copy
                                         ).then_inc(S["x_rounded"], 1)
                    nc.scalar.activation(xs.b[0:DB, :], bank(1)[0:DB, 0:WIDE], ACT.Copy
                                         ).then_inc(S["x_rounded"], 1)

            def copy_qk(i, c0, c1):
                for c in range(c0, c1):
                    act.wait_ge(S["qk_done"], 2 * chunks * i + c + 1)
                    dst_, bias, n = (q, q_bias, c) if c < chunks else (k, k_bias, c - chunks)
                    scale = q_scale if c < chunks else 1.0
                    if bias is None:
                        ins = nc.scalar.activation(dst_[n][:, :], bank(c % 2)[:, 0:WIDE], ACT.Copy,
                                                   scale=scale)
                    else:
                        ins = nc.scalar.activation(dst_[n][:, :], bank(c % 2)[:, 0:WIDE], ACT.Identity,
                                                   bias=bias[:, n:n + 1], scale=scale)
                    ins.then_inc(S["qk_evacuated"], 1)

            def copy_v(i, s):
                act.wait_ge(S["v_done"], UNITS * i + s + 1)
                if s == 0:
                    act.wait_ge(S["values_mixed"], UNITS * i)
                else:
                    act.wait_ge(S["values_mixed"], UNITS * i + s - 1)
                src_ = psum[0:UNIT, 0:z_banks * BANK].rearrange("p (b n) -> p b n", b=z_banks)[
                    :, :, 0:v_cols].rearrange("p b (h e) -> p b h e", e=dh)
                out = v[s % 2][:, :, :].rearrange("p (b h) e -> p b h e", b=z_banks)[:, :, :, 0:dh]
                nc.scalar.activation(out, src_, ACT.Copy).then_inc(S["v_evacuated"], 1)

            def exponentiate(i, s):
                for b in range(2):
                    act.wait_ge(S["scores_shifted"], 2 * (UNITS * i + s) + b + 1)
                    part = prob[s % 2][:, b * HB:(b + 1) * HB, :]
                    nc.scalar.activation(part, part, ACT.Exp).then_inc(S["exp_done"], 1)

            def copy_prob_t(i, s):
                for b in range(2):
                    act.wait_ge(S["prob_transposed"], 2 * (UNITS * i + s) + b + 1)
                    nc.scalar.activation(prob_t[:, b * HB:(b + 1) * HB, :], scores_bank(4 + b), ACT.Copy
                                         ).then_inc(S["prob_t_evacuated"], 1)

            def copy_z_t(i, s):
                act.wait_ge(S["z_transposed"], UNITS * i + s + 1)
                toks = slice(s * UNIT, (s + 1) * UNIT)
                full = [n for n, (_, m) in enumerate(z_chunks) if m == P]
                if len(full) < len(z_chunks):
                    m = z_chunks[-1][1]
                    nc.scalar.activation(z_t[0:m, len(full), toks], zt_ps[0:m, len(full), :], ACT.Copy
                                         ).then_inc(S["zt_part"], 1)
                nc.scalar.activation(z_t[:, 0:len(full), toks], zt_ps[:, 0:len(full), :], ACT.Copy
                                     ).then_inc(S["zt_evacuated"], 1)

            def body(i, last):
                copy_v(i, 0)
                exponentiate(i, 0)
                copy_v(i, 1)
                copy_prob_t(i, 0)
                exponentiate(i, 1)
                copy_v(i, 2)
                copy_z_t(i, 0)
                copy_prob_t(i, 1)
                exponentiate(i, 2)
                copy_v(i, 3)
                if not last:
                    round_x(i + 1)
                copy_z_t(i, 1)
                copy_prob_t(i, 2)
                exponentiate(i, 3)
                if not last:
                    copy_qk(i + 1, 0, chunks)
                copy_z_t(i, 2)
                copy_prob_t(i, 3)
                if not last:
                    copy_qk(i + 1, chunks, 2 * chunks)
                copy_z_t(i, 3)

            round_x(0)
            copy_qk(0, 0, 2 * chunks)
            with act.Fori(0, n_iter - 1) as i:
                body(i, False)
            body(n_iter - 1, True)

        @block.vector
        def _(dve):
            def pre_stat(i):
                dve.wait_ge(S["x_loaded"], 16 * i + 16)
                for t in range(TILES):
                    nc.vector.bn_stats(pre_stats[:, t, :], x_tok[:, t, :]).then_inc(S["pre_stats_ready"], 1)
                for t in range(TILES):
                    wait_apart(dve, S["pre_stats_ready"], TILES * i + t + 1)
                    nc.vector.bn_aggr(pre_mv[:, t, :], pre_stats[:, t, :]).then_inc(S["pre_mv_ready"], 1)
                dve.wait_ge(S["pre_mv_ready"], TILES * (i + 1))
                nc.vector.tensor_scalar(pre_var[:, :], pre_mv[:, :, 1], EPS, None, ALU.add
                                        ).then_inc(S["pre_var_ready"], 1)

            def pre_norm(i):
                dve.wait_ge(S["pre_rstd_ready"], i + 1)
                dve.wait_ge(S["x_transposed"], i)
                for t in range(TILES):
                    last = nc.vector.tensor_scalar(x_hat[:, t, :], x_tok[:, t, :], pre_mv[:, t, 0:1],
                                                   pre_rstd[:, t:t + 1], ALU.subtract, ALU.mult)
                last.then_inc(S["x_hat_ready"], 1)

            def split_x(i):
                a_ps, b_ps = bank(0)[:, 0:WIDE], bank(1)[0:DB, 0:WIDE]
                dve.wait_ge(S["x_rounded"], 2 * i + 2)
                if prenorm:
                    ga, gb, ba, bb = prenorm
                    nc.vector.tensor_scalar(x_aff_a[:, :], a_ps, ga, ba, ALU.mult, ALU.add
                                            ).then_inc(S["x_affine"], 1)
                    nc.vector.tensor_scalar(x_aff_b[:, :], b_ps, gb, bb, ALU.mult, ALU.add
                                            ).then_inc(S["x_affine"], 1)
                    dve.wait_ge(S["x_affine"], 2 * i + 2)
                    a_ps, b_ps = x_aff_a[:, :], x_aff_b[:, :]
                nc.vector.tensor_tensor(xs.a_lo[:, :], a_ps, xs.a_hi[:, :].bitcast(F32), ALU.subtract)
                nc.vector.tensor_tensor(xs.b[DB:P, :], b_ps, xs.b[0:DB, :].bitcast(F32), ALU.subtract
                                        ).then_inc(S["x_split"], 1)

            def softmax(i, s):
                u = UNITS * i + s
                if s == 0:
                    dve.wait_ge(S["prob_transposed"], 2 * u)
                else:
                    dve.wait_ge(S["prob_transposed"], 2 * (u - 1))
                pr, mx = prob[s % 2], row_max[s % 2]
                for b in range(2):
                    hs = slice(b * HB, (b + 1) * HB)
                    dve.wait_ge(S["scores_done"], 2 * u + b + 1)
                    nc.vector.tensor_tensor(pr[:, hs, :], scores_bank(2 + b), bias_hk[:, hs, :], ALU.add
                                            ).then_inc(S["scores_biased"], 1)
                for b in range(2):
                    hs = slice(b * HB, (b + 1) * HB)
                    dve.wait_ge(S["scores_biased"], 2 * u + b + 1)
                    nc.vector.tensor_reduce(mx[:, hs], pr[:, hs, :], axis=AX.X, op=ALU.max
                                            ).then_inc(S["max_done"], 1)
                for b in range(2):
                    hs = slice(b * HB, (b + 1) * HB)
                    dve.wait_ge(S["max_done"], 2 * u + b + 1)
                    nc.vector.tensor_tensor(pr[:, hs, :], pr[:, hs, :],
                                            mx[:, hs].rearrange("p (h a) -> p h a", a=1)
                                            .to_broadcast([UNIT, HB, UNIT]), ALU.subtract
                                            ).then_inc(S["scores_shifted"], 1)

            def normalise_z(i, s):
                u = UNITS * i + s
                dve.wait_ge(S["values_mixed"], u + 1)
                nc.vector.reciprocal(z_recip[:, :].rearrange("p (b h) -> p b h", b=z_banks),
                                     z_ps[:, :, :, dh]).then_inc(S["z_recip_ready"], 1)
                dve.wait_ge(S["z_recip_ready"], u + 1)
                for b in range(z_banks):
                    hs = slice(b * zh, (b + 1) * zh)
                    last = nc.vector.tensor_tensor(z[:, hs, :], z_ps[:, b, :, 0:dh],
                                                   z_recip[:, hs].rearrange("p (h a) -> p h a", a=1)
                                                   .to_broadcast([UNIT, zh, dh]), ALU.mult)
                last.then_inc(S["z_normalised"], 1)

            def add_residual(i, t):
                dve.wait_ge(S["out_done"], TILES * i + t + 1)
                dve.wait_ge(S["residual_ready"], i + 1)
                if t == 0:
                    dve.wait_ge(S["y_stored"], 16 * i)
                nc.vector.tensor_tensor(y[:, t, :], bank(4)[0:TILE, 0:D], residual[:, t, :], ALU.add
                                        ).then_inc(S["attn_added"], 1)
                if not postnorm:
                    return
                n = TILES * i + t + 1
                dve.wait_ge(S["attn_added"], n)
                nc.vector.bn_stats(stats[:, t, :], y[:, t, :]).then_inc(S["stats_ready"], 1)
                wait_apart(dve, S["stats_ready"], n)
                nc.vector.bn_aggr(mean_var[:, t, :], stats[:, t, :]).then_inc(S["mean_ready"], 1)
                dve.wait_ge(S["mean_ready"], n)
                nc.vector.tensor_scalar(var_eps[:, t:t + 1], mean_var[:, t, 1:2], EPS, None, ALU.add
                                        ).then_inc(S["var_ready"], 1)

            def post_norm(i, t):
                if not postnorm:
                    return
                dve.wait_ge(S["rstd_ready"], TILES * i + t + 1)
                nc.vector.tensor_scalar(y[:, t, :], y[:, t, :], mean_var[:, t, 0:1], rstd[:, t:t + 1],
                                        ALU.subtract, ALU.mult).then_inc(S["y_ready"], 1)

            def body(i, last):
                softmax(i, 0)
                softmax(i, 1)
                normalise_z(i, 0)
                if prenorm and not last:
                    pre_stat(i + 1)
                softmax(i, 2)
                normalise_z(i, 1)
                if prenorm and not last:
                    pre_norm(i + 1)
                softmax(i, 3)
                if not last:
                    split_x(i + 1)
                normalise_z(i, 2)
                add_residual(i, 0)
                normalise_z(i, 3)
                post_norm(i, 0)
                add_residual(i, 1)
                post_norm(i, 1)
                add_residual(i, 2)
                post_norm(i, 2)

            if prenorm:
                pre_stat(0)
                pre_norm(0)
            split_x(0)
            with dve.Fori(0, n_iter - 1) as i:
                body(i, False)
            body(n_iter - 1, True)



def mlp_stage(nc, psum, ident, neg_half, name, h_src, x_src, dst, n_iter, w_up, b_up, branches,
              out_bias, prenorm):
    chunks = HID // P
    per_iter = chunks * len(branches)
    with Sems(nc, name) as S, ExitStack() as ctx:
        def sb(nm, shape, dt=F32):
            return ctx.enter_context(nc.sbuf_tensor(f"{name}_{nm}", shape, dt))

        h_tok, x_tok, x_hat = (sb(n, [MT, 3, D]) for n in ("h_tok", "x_tok", "x_hat"))
        residual, y = sb("residual", [MT, 3, D]), sb("y", [MT, 3, D])
        res_part = sb("res_part", [MT, 3, D])
        xs = SplitX(sb, "x", MW)
        x_aff_a, x_aff_b = sb("x_aff_a", [P, MW]), sb("x_aff_b", [DB, MW])
        hid = [sb(f"hid{p}", [P, chunks, MW]) for p in range(min(2, len(branches)))]
        pre_stats, stats = sb("pre_stats", [MT, 3, 6]), sb("stats", [MT, 3, 6])
        pre_mv, mean_var = sb("pre_mv", [MT, 3, 2]), sb("mean_var", [MT, 3, 2])
        pre_var, pre_rstd, var_eps, rstd = (sb(n, [MT, 3]) for n in ("pre_var", "pre_rstd", "var_eps", "rstd"))

        def bank(b):
            return psum[:, b * BANK:(b + 1) * BANK]

        block = ctx.enter_context(nc.Block())

        @block.sync
        def _(sp):
            def load(i):
                sp.wait_ge(S["residual_ready"], i)
                sp.wait_ge(S["x_hat_ready"], i)
                sp.dma_start(x_tok[:, :, :], x_src(i)).then_inc(S["x_loaded"], 16)
                sp.dma_start(h_tok[:, :, :], h_src(i)).then_inc(S["h_loaded"], 16)

            def store(i):
                sp.wait_ge(S["y_ready"], 3 * i + 3)
                sp.dma_start(dst(i), y[:, :, :]).then_inc(S["y_stored"], 16)

            sp.dma_start(x_tok[:, :, :], x_src(0)).then_inc(S["x_loaded"], 16)
            sp.dma_start(h_tok[:, :, :], h_src(0)).then_inc(S["h_loaded"], 16)
            with sp.Fori(0, n_iter - 1) as i:
                load(i + 1)
                store(i)
            store(n_iter - 1)
            sp.wait_ge(S["y_stored"], 16 * n_iter)

        @block.gpsimd
        def _(pool):
            def pre_pow(i):
                pool.wait_ge(S["pre_var_ready"], i + 1)
                nc.gpsimd.tensor_tensor(pre_rstd[:, :], pre_var[:, :], neg_half[:, :], ALU.pow
                                        ).then_inc(S["pre_rstd_ready"], 1)

            def make_residual(i):
                pool.wait_ge(S["x_loaded"], 16 * i + 16)
                pool.wait_ge(S["h_loaded"], 16 * i + 16)
                nc.gpsimd.tensor_tensor(res_part[:, :, :], x_tok[:, :, :], h_tok[:, :, :], ALU.add
                                        ).then_inc(S["res_part_ready"], 1)
                pool.wait_ge(S["res_part_ready"], i + 1)
                pool.wait_ge(S["mlp_added"], 3 * i)
                nc.gpsimd.tensor_tensor(residual[:, :, :], res_part[:, :, :],
                                        out_bias.rearrange("p (a n) -> p a n", a=1)
                                        .to_broadcast([MT, 3, D]), ALU.add
                                        ).then_inc(S["residual_ready"], 1)

            def out_pow(i, t):
                pool.wait_ge(S["var_ready"], 3 * i + t + 1)
                nc.gpsimd.tensor_tensor(rstd[:, t:t + 1], var_eps[:, t:t + 1], neg_half[:, 0:1], ALU.pow
                                        ).then_inc(S["rstd_ready"], 1)

            def body(i, last):
                make_residual(i)
                if not last:
                    pre_pow(i + 1)
                for t in range(3):
                    out_pow(i, t)

            pre_pow(0)
            with pool.Fori(0, n_iter - 1) as i:
                body(i, False)
            body(n_iter - 1, True)

        @block.tensor
        def _(pe):
            def transpose_x(i):
                pe.wait_ge(S["x_hat_ready"], i + 1)
                for t in range(3):
                    nc.tensor.transpose(bank(6)[:, t * MT:(t + 1) * MT], x_hat[:, t, 0:P], ident[:, :])
                    last = nc.tensor.transpose(bank(7)[0:DB, t * MT:(t + 1) * MT], x_hat[:, t, P:D],
                                               ident[:, :])
                last.then_inc(S["x_transposed"], 1)

            def up(i, br):
                kept = branches[br][0]
                for c in range(chunks):
                    n = br * chunks + c
                    if n == 0:
                        pe.wait_ge(S["x_split"], i + 1)
                        pe.wait_ge(S["gelu_done"], per_iter * i)
                    elif n >= 3:
                        pe.wait_ge(S["gelu_done"], per_iter * i + n - 2)
                    out, cols = bank(n % 3)[:, 0:MW], slice(c * P, (c + 1) * P)
                    if kept == D:
                        ins = weight_by_x(nc, out, w_up, cols, xs, slice(0, MW))
                    else:
                        ins = weight_by_x_head(nc, out, w_up, cols, xs, slice(0, MW), kept)
                    ins.then_inc(S["up_done"], 1)

            def down(i, br):
                w = branches[br][1]
                if br == 0:
                    pe.wait_ge(S["mlp_added"], 3 * i)
                final = br == len(branches) - 1
                for t in range(3):
                    for c in range(chunks):
                        if t == 0:
                            pe.wait_ge(S["gelu_done"], per_iter * i + br * chunks + c + 1)
                        last = nc.tensor.matmul(bank(3 + t)[:, 0:w.shape[2]],
                                                hid[br % 2][:, c, t * MT:(t + 1) * MT], w[:, c, :],
                                                start=(br == 0 and c == 0), stop=(final and c == chunks - 1))
                    if final:
                        last.then_inc(S["down_done"], 1)

            def body(i, last):
                up(i, 0)
                for br in range(1, len(branches)):
                    up(i, br)
                    down(i, br - 1)
                if not last:
                    transpose_x(i + 1)
                down(i, len(branches) - 1)

            transpose_x(0)
            with pe.Fori(0, n_iter - 1) as i:
                body(i, False)
            body(n_iter - 1, True)

        @block.scalar
        def _(act):
            def round_x(i):
                act.wait_ge(S["x_transposed"], i + 1)
                ga, gb, ba, bb = prenorm
                nc.scalar.activation(xs.a_hi[:, :], bank(6)[:, 0:MW], ACT.Identity, bias=ba, scale=ga
                                     ).then_inc(S["x_rounded"], 1)
                nc.scalar.activation(xs.b[0:DB, :], bank(7)[0:DB, 0:MW], ACT.Identity, bias=bb, scale=gb
                                     ).then_inc(S["x_rounded"], 1)

            def gelu(i):
                for n in range(per_iter):
                    act.wait_ge(S["up_done"], per_iter * i + n + 1)
                    c = n % chunks
                    nc.scalar.activation(hid[(n // chunks) % 2][:, c, :], bank(n % 3)[:, 0:MW], ACT.Gelu,
                                         bias=b_up[:, c:c + 1]).then_inc(S["gelu_done"], 1)

            round_x(0)
            with act.Fori(0, n_iter - 1) as i:
                gelu(i)
                round_x(i + 1)
            gelu(n_iter - 1)

        @block.vector
        def _(dve):
            def pre_norm(i):
                dve.wait_ge(S["x_loaded"], 16 * i + 16)
                for t in range(3):
                    nc.vector.bn_stats(pre_stats[:, t, :], x_tok[:, t, :]).then_inc(S["pre_stats_ready"], 1)
                for t in range(3):
                    wait_apart(dve, S["pre_stats_ready"], 3 * i + t + 1)
                    nc.vector.bn_aggr(pre_mv[:, t, :], pre_stats[:, t, :]).then_inc(S["pre_mv_ready"], 1)
                dve.wait_ge(S["pre_mv_ready"], 3 * i + 3)
                nc.vector.tensor_scalar(pre_var[:, :], pre_mv[:, :, 1], EPS, None, ALU.add
                                        ).then_inc(S["pre_var_ready"], 1)
                dve.wait_ge(S["pre_rstd_ready"], i + 1)
                dve.wait_ge(S["x_transposed"], i)
                for t in range(3):
                    last = nc.vector.tensor_scalar(x_hat[:, t, :], x_tok[:, t, :], pre_mv[:, t, 0:1],
                                                   pre_rstd[:, t:t + 1], ALU.subtract, ALU.mult)
                last.then_inc(S["x_hat_ready"], 1)

            def split_x(i):
                ga, gb, ba, bb = prenorm
                dve.wait_ge(S["x_rounded"], 2 * i + 2)
                nc.vector.tensor_scalar(x_aff_a[:, :], bank(6)[:, 0:MW], ga, ba, ALU.mult, ALU.add
                                        ).then_inc(S["x_affine"], 1)
                nc.vector.tensor_scalar(x_aff_b[:, :], bank(7)[0:DB, 0:MW], gb, bb, ALU.mult, ALU.add
                                        ).then_inc(S["x_affine"], 1)
                dve.wait_ge(S["x_affine"], 2 * i + 2)
                nc.vector.tensor_tensor(xs.a_lo[:, :], x_aff_a[:, :], xs.a_hi[:, :].bitcast(F32),
                                        ALU.subtract)
                nc.vector.tensor_tensor(xs.b[DB:P, :], x_aff_b[:, :], xs.b[0:DB, :].bitcast(F32),
                                        ALU.subtract).then_inc(S["x_split"], 1)

            def add_residual(i, t):
                n = 3 * i + t + 1
                dve.wait_ge(S["down_done"], n)
                if t == 0:
                    dve.wait_ge(S["residual_ready"], i + 1)
                    dve.wait_ge(S["y_stored"], 16 * i)
                nc.vector.tensor_tensor(y[:, t, :], bank(3 + t)[:, 0:D], residual[:, t, :], ALU.add
                                        ).then_inc(S["mlp_added"], 1)
                dve.wait_ge(S["mlp_added"], n)
                nc.vector.bn_stats(stats[:, t, :], y[:, t, :]).then_inc(S["stats_ready"], 1)
                wait_apart(dve, S["stats_ready"], n)
                nc.vector.bn_aggr(mean_var[:, t, :], stats[:, t, :]).then_inc(S["mean_ready"], 1)
                dve.wait_ge(S["mean_ready"], n)
                nc.vector.tensor_scalar(var_eps[:, t:t + 1], mean_var[:, t, 1:2], EPS, None, ALU.add
                                        ).then_inc(S["var_ready"], 1)

            def post_norm(i, t):
                dve.wait_ge(S["rstd_ready"], 3 * i + t + 1)
                nc.vector.tensor_scalar(y[:, t, :], y[:, t, :], mean_var[:, t, 0:1], rstd[:, t:t + 1],
                                        ALU.subtract, ALU.mult).then_inc(S["y_ready"], 1)

            def body(i, last):
                if not last:
                    pre_norm(i + 1)
                    split_x(i + 1)
                add_residual(i, 0)
                add_residual(i, 1)
                post_norm(i, 0)
                add_residual(i, 2)
                post_norm(i, 1)
                post_norm(i, 2)

            pre_norm(0)
            split_x(0)
            with dve.Fori(0, n_iter - 1) as i:
                body(i, False)
            body(n_iter - 1, True)



def moe_stage(nc, psum, ident, neg_half, name, src, dst, n_iter, w_gu, w_router, sg_bias, w_dn_shared,
              w_dn, w_dn_mid, iota8):
    sh = HID // P
    pair = 2 * D // P
    groups = [(0, sh)] + [(sh + pair * n, pair) for n in range(EXPERTS // 2)]
    total = sh + EH // P
    outs = 3 * (1 + EXPERTS)

    def gate_col(c):
        return c * P if c < sh else 2 * HID + (c - sh) * P

    def up_col(c):
        return HID + c * P if c < sh else 2 * HID + EH + (c - sh) * P

    with Sems(nc, name) as S, ExitStack() as ctx:
        def sb(nm, shape, dt=F32):
            return ctx.enter_context(nc.sbuf_tensor(f"{name}_{nm}", shape, dt))

        h_tok, acc, y = (sb(n, [MT, 3, D]) for n in ("h_tok", "acc", "y"))
        xs = SplitX(sb, "x", MW)
        silu = [sb(f"silu{p}", [P, MW]) for p in range(2)]
        hid_shared = sb("hid_shared", [P, sh, MW])
        hid_pair = [sb(f"hid_pair{p}", [P, pair, MW]) for p in range(2)]
        logits = sb("logits", [MT, 3, 10])
        top8 = sb("top8", [MT, 3, 8])
        index = sb("index", [MT, 3, 8], U32)
        index_f = sb("index_f", [MT, 3, 2])
        pre_tanh, tanh = sb("pre_tanh", [MT, 2, 3]), sb("tanh", [MT, 2, 3])
        plus, minus = sb("plus", [MT, 2, 3]), sb("minus", [MT, 2, 3])
        gate1, gate2 = sb("gate1", [MT, 3]), sb("gate2", [MT, 3])
        coef1, coef = sb("coef1", [MT, 3, 8]), sb("coef", [MT, 3, 8])
        alpha = sb("alpha", [MT, 3])
        stats, mean_var = sb("stats", [MT, 3, 6]), sb("mean_var", [MT, 3, 2])
        var_eps, rstd = sb("var_eps", [MT, 3]), sb("rstd", [MT, 3])

        def hid(gr):
            return hid_shared if gr == 0 else hid_pair[(gr - 1) % 2]

        def bank(b):
            return psum[:, b * BANK:(b + 1) * BANK]

        block = ctx.enter_context(nc.Block())

        @block.sync
        def _(sp):
            def load_next(i):
                sp.wait_ge(S["x_transposed"], i + 1)
                sp.wait_ge(S["combined"], outs * i + 3)
                sp.dma_start(h_tok[:, :, :], src(i + 1)).then_inc(S["h_loaded"], 16)

            def store(i):
                sp.wait_ge(S["y_ready"], 3 * i + 3)
                sp.dma_start(dst(i), y[:, :, :]).then_inc(S["y_stored"], 16)

            sp.dma_start(h_tok[:, :, :], src(0)).then_inc(S["h_loaded"], 16)
            with sp.Fori(0, n_iter - 1) as i:
                load_next(i)
                store(i)
            store(n_iter - 1)
            sp.wait_ge(S["y_stored"], 16 * n_iter)

        @block.gpsimd
        def _(pool):
            with pool.Fori(0, n_iter) as i:
                for t in range(3):
                    pool.wait_ge(S["var_ready"], 3 * i + t + 1)
                    nc.gpsimd.tensor_tensor(rstd[:, t:t + 1], var_eps[:, t:t + 1], neg_half[:, 0:1],
                                            ALU.pow).then_inc(S["rstd_ready"], 1)

        @block.tensor
        def _(pe):
            def transpose_x(i):
                pe.wait_ge(S["h_loaded"], 16 * i + 16)
                pe.wait_ge(S["logits_copied"], i)
                for t in range(3):
                    nc.tensor.transpose(bank(6)[:, t * MT:(t + 1) * MT], h_tok[:, t, 0:P], ident[:, :])
                    last = nc.tensor.transpose(bank(7)[0:DB, t * MT:(t + 1) * MT], h_tok[:, t, P:D],
                                               ident[:, :])
                last.then_inc(S["x_transposed"], 1)

            def route(i):
                pe.wait_ge(S["x_split"], i + 1)
                for t in range(3):
                    last = x_by_weight(nc, bank(6)[:, t * 10:t * 10 + 10], xs, slice(t * MT, (t + 1) * MT),
                                       w_router, slice(0, 10))
                last.then_inc(S["logits_done"], 1)

            def gate_up(i, gr):
                first, count = groups[gr]
                for c in range(first, first + count):
                    if c == 0:
                        pe.wait_ge(S["x_split"], i + 1)
                    if c >= 2:
                        pe.wait_ge(S["hid_ready"], total * i + c - 1)
                    else:
                        pe.wait_ge(S["hid_ready"], total * i)
                    b = 2 * (c % 2)
                    weight_by_x(nc, bank(b)[:, 0:MW], w_gu, slice(gate_col(c), gate_col(c) + P), xs,
                                slice(0, MW)).then_inc(S["gate_done"], 1)
                    weight_by_x(nc, bank(b + 1)[:, 0:MW], w_gu, slice(up_col(c), up_col(c) + P), xs,
                                slice(0, MW)).then_inc(S["up_done"], 1)

            def down(i, gr):
                first, count = groups[gr]
                pe.wait_ge(S["hid_ready"], total * i + first + count)
                if gr == 0:
                    sums = [[(c, w_dn_shared[:, c, :]) for c in range(sh)]]
                else:
                    k = gr - 1
                    sums = [[(0, w_dn[:, 3 * k, :]), (1, w_dn_mid[:, 2 * k, :])],
                            [(1, w_dn_mid[:, 2 * k + 1, :]), (2, w_dn[:, 3 * k + 2, :])]]
                for e, terms in enumerate(sums):
                    for t in range(3):
                        n = 3 * (0 if gr == 0 else 2 * gr - 1 + e) + t
                        if n >= 2:
                            pe.wait_ge(S["combined"], outs * i + n - 1)
                        else:
                            pe.wait_ge(S["combined"], outs * i)
                        for m, (c, w) in enumerate(terms):
                            last = nc.tensor.matmul(bank(4 + n % 2)[:, 0:D],
                                                    hid(gr)[:, c, t * MT:(t + 1) * MT], w,
                                                    start=(m == 0), stop=(m == len(terms) - 1))
                        last.then_inc(S["down_done"], 1)

            def body(i, last):
                gate_up(i, 0)
                gate_up(i, 1)
                down(i, 0)
                gate_up(i, 2)
                down(i, 1)
                gate_up(i, 3)
                down(i, 2)
                gate_up(i, 4)
                if not last:
                    transpose_x(i + 1)
                down(i, 3)
                if not last:
                    route(i + 1)
                down(i, 4)

            transpose_x(0)
            route(0)
            with pe.Fori(0, n_iter - 1) as i:
                body(i, False)
            body(n_iter - 1, True)

        @block.scalar
        def _(act):
            def round_x(i):
                act.wait_ge(S["x_transposed"], i + 1)
                nc.scalar.activation(xs.a_hi[:, :], bank(6)[:, 0:MW], ACT.Copy).then_inc(S["x_rounded"], 1)
                nc.scalar.activation(xs.b[0:DB, :], bank(7)[0:DB, 0:MW], ACT.Copy
                                     ).then_inc(S["x_rounded"], 1)

            def gates(i):
                act.wait_ge(S["pre_tanh_ready"], 2 * i + 2)
                nc.scalar.activation(tanh[:, :, :], pre_tanh[:, :, :], ACT.Tanh, scale=0.5
                                     ).then_inc(S["tanh_ready"], 1)

            def silus(i):
                for c in range(total):
                    act.wait_ge(S["gate_done"], total * i + c + 1)
                    if c >= 2:
                        act.wait_ge(S["hid_ready"], total * i + c - 1)
                    nc.scalar.activation(silu[c % 2][:, :], bank(2 * (c % 2))[:, 0:MW], ACT.Silu
                                         ).then_inc(S["silu_done"], 1)

            round_x(0)
            gates(0)
            with act.Fori(0, n_iter - 1) as i:
                silus(i)
                round_x(i + 1)
                gates(i + 1)
            silus(n_iter - 1)

        @block.vector
        def _(dve):
            def split_x(i):
                dve.wait_ge(S["x_rounded"], 2 * i + 2)
                nc.vector.tensor_tensor(xs.a_lo[:, :], bank(6)[:, 0:MW], xs.a_hi[:, :].bitcast(F32),
                                        ALU.subtract)
                nc.vector.tensor_tensor(xs.b[DB:P, :], bank(7)[0:DB, 0:MW], xs.b[0:DB, :].bitcast(F32),
                                        ALU.subtract).then_inc(S["x_split"], 1)

            def gates(i):
                dve.wait_ge(S["logits_done"], i + 1)
                nc.vector.tensor_copy(logits[:, :, :], bank(6)[:, 0:30].rearrange("p (t n) -> p t n", t=3)
                                      ).then_inc(S["logits_copied"], 1)
                dve.wait_ge(S["logits_copied"], i + 1)
                nc.vector.tensor_scalar(pre_tanh[:, 1, :], logits[:, :, 8], sg_bias, None, ALU.add
                                        ).then_inc(S["pre_tanh_ready"], 1)
                for t in range(3):
                    nc.vector.max(top8[:, t, :], logits[:, t, 0:8]).then_inc(S["top_ready"], 1)
                dve.wait_ge(S["top_ready"], 3 * i + 3)
                nc.vector.tensor_tensor(pre_tanh[:, 0, :], top8[:, :, 0], top8[:, :, 1], ALU.subtract
                                        ).then_inc(S["pre_tanh_ready"], 1)
                for t in range(3):
                    nc.vector.max_index(index[:, t, :], top8[:, t, :], logits[:, t, 0:8]
                                        ).then_inc(S["index_ready"], 1)
                dve.wait_ge(S["index_ready"], 3 * i + 3)
                nc.vector.tensor_copy(index_f[:, :, :], index[:, :, 0:2]).then_inc(S["index_f_ready"], 1)
                dve.wait_ge(S["tanh_ready"], i + 1)
                nc.vector.tensor_scalar(plus[:, :, :], tanh[:, :, :], 0.5, 0.5, ALU.mult, ALU.add
                                        ).then_inc(S["sigmoids_ready"], 1)
                nc.vector.tensor_scalar(minus[:, :, :], tanh[:, :, :], -0.5, 0.5, ALU.mult, ALU.add
                                        ).then_inc(S["sigmoids_ready"], 1)
                dve.wait_ge(S["sigmoids_ready"], 2 * i + 2)
                nc.vector.tensor_copy(alpha[:, :], plus[:, 1, :]).then_inc(S["gates_ready"], 1)
                nc.vector.tensor_tensor(gate1[:, :], plus[:, 0, :], minus[:, 1, :], ALU.mult
                                        ).then_inc(S["gates_ready"], 1)
                nc.vector.tensor_tensor(gate2[:, :], minus[:, 0, :], minus[:, 1, :], ALU.mult
                                        ).then_inc(S["gates_ready"], 1)
                dve.wait_ge(S["gates_ready"], 3 * i + 3)
                dve.wait_ge(S["index_f_ready"], i + 1)
                for t in range(3):
                    nc.vector.tensor_scalar(coef1[:, t, :], iota8, index_f[:, t, 0:1], gate1[:, t:t + 1],
                                            ALU.is_equal, ALU.mult).then_inc(S["coef_parts_ready"], 1)
                    nc.vector.tensor_scalar(coef[:, t, :], iota8, index_f[:, t, 1:2], gate2[:, t:t + 1],
                                            ALU.is_equal, ALU.mult).then_inc(S["coef_parts_ready"], 1)
                dve.wait_ge(S["coef_parts_ready"], 6 * i + 6)
                nc.vector.tensor_tensor(coef[:, :, :], coef[:, :, :], coef1[:, :, :], ALU.add
                                        ).then_inc(S["coef_ready"], 1)
                dve.wait_ge(S["coef_ready"], i + 1)

            def multiply(i, gr):
                first, count = groups[gr]
                for c in range(first, first + count):
                    dve.wait_ge(S["silu_done"], total * i + c + 1)
                    dve.wait_ge(S["up_done"], total * i + c + 1)
                    nc.vector.tensor_tensor(hid(gr)[:, c - first, :], bank(2 * (c % 2) + 1)[:, 0:MW],
                                            silu[c % 2][:, :], ALU.mult).then_inc(S["hid_ready"], 1)

            def combine(i, gr):
                for e in ([0] if gr == 0 else [2 * gr - 1, 2 * gr]):
                    for t in range(3):
                        n = 3 * e + t
                        dve.wait_ge(S["down_done"], outs * i + n + 1)
                        if e > 0:
                            dve.wait_ge(S["combined"], outs * i + n - 2)
                        scalar = alpha[:, t:t + 1] if e == 0 else coef[:, t, e - 1:e]
                        ins = nc.vector.scalar_tensor_tensor(
                            out=acc[:, t, :], in0=bank(4 + n % 2)[:, 0:D], scalar=scalar,
                            in1=(h_tok if e == 0 else acc)[:, t, :], op0=ALU.mult, op1=ALU.add)
                        ins.then_inc(S["combined"], 1)

            def normalise(i):
                dve.wait_ge(S["combined"], outs * i + outs)
                for t in range(3):
                    nc.vector.bn_stats(stats[:, t, :], acc[:, t, :]).then_inc(S["stats_ready"], 1)
                for t in range(3):
                    wait_apart(dve, S["stats_ready"], 3 * i + t + 1)
                    nc.vector.bn_aggr(mean_var[:, t, :], stats[:, t, :]).then_inc(S["mean_ready"], 1)
                for t in range(3):
                    dve.wait_ge(S["mean_ready"], 3 * i + t + 1)
                    nc.vector.tensor_scalar(var_eps[:, t:t + 1], mean_var[:, t, 1:2], EPS, None, ALU.add
                                            ).then_inc(S["var_ready"], 1)
                dve.wait_ge(S["y_stored"], 16 * i)
                for t in range(3):
                    dve.wait_ge(S["rstd_ready"], 3 * i + t + 1)
                    nc.vector.tensor_scalar(y[:, t, :], acc[:, t, :], mean_var[:, t, 0:1], rstd[:, t:t + 1],
                                            ALU.subtract, ALU.mult).then_inc(S["y_ready"], 1)

            def body(i, last):
                multiply(i, 0)
                multiply(i, 1)
                combine(i, 0)
                multiply(i, 2)
                combine(i, 1)
                multiply(i, 3)
                combine(i, 2)
                multiply(i, 4)
                if not last:
                    split_x(i + 1)
                combine(i, 3)
                combine(i, 4)
                if not last:
                    gates(i + 1)
                normalise(i)

            split_x(0)
            gates(0)
            with dve.Fori(0, n_iter - 1) as i:
                body(i, False)
            body(n_iter - 1, True)



def padded(cols, width, pad):
    return cols.rearrange("p (h r) -> p h r", r=pad)[:, :, 0:width]


def split_views(w, at, n, width=None, pad=None):
    out = [t[:, at:at + n] for t in (w.a_hi, w.a_lo, w.b_hi, w.b_lo)]
    return [padded(t, width, pad) for t in out] if pad else out


def part_views(src, first, n, width):
    cols = src[:, first:first + n]
    return cols.rearrange("p (h e) -> p h e", e=width) if width else cols


def remainder_weight_jobs(nc, which, eng, S, stage_a, stage_b, jobs):
    for j, (_, n, parts) in enumerate(jobs):
        for stage, view, p in ((stage_a, 0, P), (stage_b, 2, DB)):
            eng.wait_ge(S["weight_hi_done"], 2 * j + (2 if view else 1))
            for first, count, views, width in parts:
                last = which.tensor_tensor(views[view + 1],
                                           part_views(stage[j % 2], first, count, width)[0:p],
                                           views[view][0:p].bitcast(F32), ALU.subtract)
            last.then_inc(S["weight_lo_done"], 1)


def load_one(eng, S, stage_a, stage_b, jobs, j):
    dram, n, _ = jobs[j]
    if j >= 2:
        eng.wait_ge(S["weight_lo_done"], 2 * (j - 1))
    eng.dma_start(stage_a[j % 2][:, 0:n], dram[0:P]).then_inc(S["weight_loaded%d" % (j % 2)], 16)
    for half in range(2):
        eng.dma_start(stage_b[j % 2][half * DB:(half + 1) * DB, 0:n], dram[P:D]
                      ).then_inc(S["weight_loaded%d" % (j % 2)], 16)


def round_one(nc, eng, S, stage_a, stage_b, jobs, j):
    _, n, parts = jobs[j]
    eng.wait_ge(S["weight_loaded%d" % (j % 2)], 48 * (j // 2 + 1))
    if j == 0:
        eng.wait_ge(S["pads_cleared"], PADS)
    for stage, view in ((stage_a, 0), (stage_b, 2)):
        for first, count, views, width in parts:
            last = nc.scalar.activation(views[view], part_views(stage[j % 2], first, count, width),
                                        ACT.Copy)
        last.then_inc(S["weight_hi_done"], 1)


def embed_stage(nc, psum, name, patches_t, w_tok, w_tok_dram, pos_rows, b_rows, dst, jobs,
                prepare):
    n_iter, chunks = TOK // WIDE, PATCH_K // P
    with Sems(nc, name) as S, ExitStack() as ctx:
        def sb(nm, shape, dt=F32):
            return ctx.enter_context(nc.sbuf_tensor(f"{name}_{nm}", shape, dt))

        patches = [sb(f"patches{p}", [P, chunks, WIDE]) for p in range(2)]
        pos = sb("pos", [TILE, TILES, D])
        b_tok = sb("b_tok", [TILE, D])
        pos_b = sb("pos_b", [TILE, TILES, D])
        y = [sb(f"y{p}", [TILE, TILES, D]) for p in range(2)]
        stage_a = [sb(f"stage_a{p}", [P, 768]) for p in range(2)]
        stage_b = [sb(f"stage_b{p}", [P, 768]) for p in range(2)]

        def out_bank(n):
            return psum[0:TILE, n * BANK:n * BANK + D]

        prep = prepare(S, sb)
        block = ctx.enter_context(nc.Block())

        @block.sync
        def _(sp):
            sp.dma_start(w_tok[:, :, :], w_tok_dram).then_inc(S["tok_weights_loaded"], 16)
            sp.dma_start(pos[:, :, :], pos_rows).then_inc(S["pos_loaded"], 16)
            sp.dma_start(b_tok[:, :], b_rows).then_inc(S["pos_loaded"], 16)
            sp.dma_start(patches[0][:, :, :], patches_t(0)).then_inc(S["patches_loaded0"], 16)

            def step(i, p, last):
                if not last:
                    sp.wait_ge(S["embedded"], TILES * i)
                    sp.dma_start(patches[1 - p][:, :, :], patches_t(i + 1)
                                 ).then_inc(S[f"patches_loaded{1 - p}"], 16)
                sp.wait_ge(S["y_ready"], TILES * (i + 1))
                sp.dma_start(dst(i), y[p][:, :, :]).then_inc(S[f"y_stored{p}"], 16)

            with sp.Fori(0, n_iter // 2 - 1) as j:
                step(2 * j, 0, False)
                step(2 * j + 1, 1, False)
            step(n_iter - 2, 0, False)
            step(n_iter - 1, 1, True)
            sp.wait_ge(S["y_stored0"], 16 * (n_iter // 2))
            sp.wait_ge(S["y_stored1"], 16 * (n_iter // 2))
            prep["sync"](sp)

        @block.tensor
        def _(pe):
            pe.wait_ge(S["tok_weights_loaded"], 16)

            def step(j, p):
                i = 2 * j + p
                pe.wait_ge(S[f"patches_loaded{p}"], 16 * j + 16)
                for t in range(TILES):
                    pe.wait_ge(S["y_ready"], TILES * i)
                    for c in range(chunks):
                        last = nc.tensor.matmul(out_bank(t), patches[p][:, c, t * TILE:(t + 1) * TILE],
                                                w_tok[:, c, :], start=(c == 0), stop=(c == chunks - 1))
                    last.then_inc(S["embedded"], 1)

            with pe.Fori(0, n_iter // 2) as j:
                step(j, 0)
                step(j, 1)
            prep["tensor"](pe)

        @block.vector
        def _(dve):
            dve.wait_ge(S["pos_loaded"], 32)
            nc.vector.tensor_tensor(pos_b[:, :, :], pos[:, :, :],
                                    b_tok[:, :].rearrange("p (a n) -> p a n", a=1)
                                    .to_broadcast([TILE, TILES, D]), ALU.add
                                    ).then_inc(S["pos_bias_ready"], 1)
            dve.wait_ge(S["pos_bias_ready"], 1)

            def step(j, p):
                i = 2 * j + p
                dve.wait_ge(S[f"y_stored{p}"], 16 * j)
                for t in range(TILES):
                    dve.wait_ge(S["embedded"], TILES * i + t + 1)
                    nc.vector.tensor_tensor(y[p][:, t, :], out_bank(t), pos_b[:, t, :], ALU.add
                                            ).then_inc(S["y_ready"], 1)

            with dve.Fori(0, n_iter // 2) as j:
                step(j, 0)
                step(j, 1)
            prep["vector"](dve)

        @block.scalar
        def _(act):
            for j in range(2):
                load_one(act, S, stage_a, stage_b, jobs, j)
            prep["scalar_loads"](act)
            for j in range(len(jobs)):
                round_one(nc, act, S, stage_a, stage_b, jobs, j)
                if j + 2 < len(jobs):
                    load_one(act, S, stage_a, stage_b, jobs, j + 2)
            prep["scalar"](act)

        @block.gpsimd
        def _(pool):
            prep["gpsimd"](pool)
            remainder_weight_jobs(nc, nc.gpsimd, pool, S, stage_a, stage_b, jobs)


class MoeWeights:

    STEPS = TOK // WIDE

    def __init__(self, nc, ctx, sb, w_gu, w_gu_dram, w_dn_shared, ws_down, w_dn, w_down, w_dn_mid):
        self.nc, self.w_gu, self.w_gu_dram = nc, w_gu, w_gu_dram
        self.n = w_gu.n // self.STEPS
        self.raw_a, self.raw_b = sb("raw_a", [P, self.n]), sb("raw_b", [P, self.n])
        self.down = (w_dn_shared, ws_down, w_dn, w_down, w_dn_mid)
        self.raw_loaded = ctx.enter_context(nc.semaphore("moe_raw_loaded"))
        self.down_loaded = ctx.enter_context(nc.semaphore("moe_down_loaded"))
        self.cleared = ctx.enter_context(nc.semaphore("moe_mid_cleared"))
        self.rounded = ctx.enter_context(nc.semaphore("moe_rounded"))
        self.split = ctx.enter_context(nc.semaphore("moe_split"))

    def load_start(self, sp):
        w_dn_shared, ws_down, w_dn, w_down, w_dn_mid = self.down
        chunks = w_down.rearrange("(c p) n -> c p n", p=P)
        sp.dma_start(w_dn_shared[:, :, :], ws_down.rearrange("(c p) n -> p c n", p=P)
                     ).then_inc(self.down_loaded, 16)
        sp.dma_start(w_dn[:, :, :], chunks.rearrange("c p n -> p c n")).then_inc(self.down_loaded, 16)
        sp.wait_ge(self.cleared, 1)
        for k in range(EXPERTS // 2):
            for half in range(2):
                rows_ = slice(half * DB, (half + 1) * DB)
                sp.dma_start(w_dn_mid[rows_, 2 * k + half, :], chunks[3 * k + 1][rows_]
                             ).then_inc(self.down_loaded, 16)
        sp.wait_ge(self.down_loaded, 16 * (2 + EXPERTS))

    def load_step(self, sp, i):
        sp.wait_ge(self.split, 2 * i)
        cols = bass.ds(i * self.n, self.n)
        sp.dma_start(self.raw_a[:, :], self.w_gu_dram[0:P, cols]).then_inc(self.raw_loaded, 16)
        for half in range(2):
            sp.dma_start(self.raw_b[half * DB:(half + 1) * DB, :], self.w_gu_dram[P:D, cols]
                         ).then_inc(self.raw_loaded, 16)

    def split_start(self, pool):
        self.nc.gpsimd.memset(self.down[4][:, :, :], 0.0).then_inc(self.cleared, 1)

    def split_step(self, pool, i):
        nc, w, cols = self.nc, self.w_gu, bass.ds(i * self.n, self.n)
        pool.wait_ge(self.raw_loaded, 48 * i + 48)
        nc.gpsimd.tensor_copy(w.a_hi[:, cols], self.raw_a[:, :]).then_inc(self.rounded, 1)
        nc.gpsimd.tensor_copy(w.b_hi[:, cols], self.raw_b[:, :]).then_inc(self.rounded, 1)
        pool.wait_ge(self.rounded, 2 * i + 2)
        nc.gpsimd.tensor_tensor(w.a_lo[:, cols], self.raw_a[:, :], w.a_hi[:, cols].bitcast(F32),
                                ALU.subtract).then_inc(self.split, 1)
        nc.gpsimd.tensor_tensor(w.b_lo[:, cols], self.raw_b[0:DB, :], w.b_hi[0:DB, cols].bitcast(F32),
                                ALU.subtract).then_inc(self.split, 1)


PADS = 16


def build(nc, x, tok_w, tok_b, pos, wq1, bq1, wk1, bk1, wv1, bv1, wo1, bo1, gumbel,
          n1l_g, n1l_b, n1s_g, n1s_b, w_qkv2, w_proj2, b_proj2, n2l_g, n2l_b, n2s_g, n2s_b,
          w_fc1, b_fc1, w_fc2, b_fc2, w_qkv3, b_qkv3, w_proj3, b_proj3,
          w_gu_dram, w_router_dram, w_down, ws_down, sg_b, out):
    top = ExitStack()
    h = [nc.dram_tensor(f"h{i}", [TOK, D], F32, kind="Internal").ap() for i in range(4)]
    x1 = nc.dram_tensor("x1", [TOK, D], F32, kind="Internal").ap()
    def tiles(a, p, first=0):
        view = a.rearrange("(i t p) d -> i p t d", t=3, p=p)
        return lambda i: view[i + first]

    with top:
        def sb(nm, shape, dt=F32):
            return top.enter_context(nc.sbuf_tensor(nm, shape, dt))

        psum = top.enter_context(nc.psum_tensor("psum", [P, 8 * BANK], F32))
        ident = sb("ident", [P, P])
        neg_half = sb("neg_half", [P, TILES])
        g = sb("gumbel", [P, 3])
        norm_a, norm_b = sb("norm_a", [P, 8]), sb("norm_b", [DB, 8])
        w_o3 = sb("w_o3", [P, 2, D])
        bias3 = sb("bias3", [UNIT, HEADS, UNIT])
        q_bias3, k_bias3 = sb("q_bias3", [P, 3]), sb("k_bias3", [P, 3])
        out_bias3 = sb("out_bias3", [TILE, D])
        w_router = Split(sb, "w_router", 10)
        sg_bias = sb("sg_bias", [P, 1])
        iota8 = sb("iota8", [P, EXPERTS])
        w_q3, w_k3, w_v3 = Split(sb, "w_q3", 384), Split(sb, "w_k3", 384), Split(sb, "w_v3", D)

        with ExitStack() as early:
            def esb(nm, shape, dt=F32):
                return early.enter_context(nc.sbuf_tensor(nm, shape, dt))

            w_tok = esb("w_tok", [P, 6, D])
            w_o1, w_o2, w_o2s = esb("w_o1", [P, 6, D]), esb("w_o2", [P, 2, D]), esb("w_o2s", [P, 2, D])
            bias1, bias2 = (esb(f"bias{n}", [UNIT, HEADS, UNIT]) for n in (1, 2))
            q_bias1, k_bias1 = esb("q_bias1", [P, 6]), esb("k_bias1", [P, 6])
            out_bias1, out_bias2, out_bias2s = (esb(f"out_bias{n}", [TILE, D]) for n in ("1", "2", "2s"))
            w_q1, w_k1, w_v1 = (Split(esb, n, HID) for n in ("w_q1", "w_k1", "w_v1"))
            w_q2, w_k2, w_v2 = Split(esb, "w_q2", 384), Split(esb, "w_k2", 384), Split(esb, "w_v2", D)
            w_up2 = Split(esb, "w_up2", HID)
            b_up2 = esb("b_up2", [P, 6])
            w_dn2 = esb("w_dn2", [P, 6, D])
            w_dn2s = [esb(f"w_dn2s{n}", [P, 6, D // (n + 1)]) for n in range(3)]
            b_dn2, b_dn2s = esb("b_dn2", [P, D]), esb("b_dn2s", [P, D])

            def plain(w, n):
                return [(0, n, split_views(w, 0, n), None)]

            def qkv_parts(wq, wk, wv):
                return [(0, D, split_views(wq, 0, 384, 16, 32), 16),
                        (D, D, split_views(wk, 0, 384, 16, 32), 16),
                        (2 * D, D, split_views(wv, 0, D), None)]

            jobs = [(wq1, HID, plain(w_q1, HID)), (wk1, HID, plain(w_k1, HID)),
                    (wv1, HID, plain(w_v1, HID)), (w_qkv2, 3 * D, qkv_parts(w_q2, w_k2, w_v2)),
                    (w_fc1, HID, plain(w_up2, HID)), (w_qkv3, 3 * D, qkv_parts(w_q3, w_k3, w_v3)),
                    (w_router_dram, 10, plain(w_router, 10))]

            def prepare(S, ssb):
                bv_cols1, bv_cols3 = ssb("bv_cols1", [P, 6]), ssb("bv_cols3", [P, 2])
                distance = ssb("distance", [UNIT, UNIT])
                distance_neg = ssb("distance_neg", [UNIT, UNIT])
                loads = []

                def load(dst, src):
                    loads.append((dst, src))

                load(g[:, :], rows(gumbel, P))
                load(sg_bias[:, :], rows(sg_b, P))
                for n, (va, vb) in enumerate(zip((n1l_g, n1l_b, n1s_g, n1s_b, n2l_g, n2l_b, n2s_g, n2s_b),
                                                 range(8))):
                    load(norm_a[:, n:n + 1], column(va[0:P]))
                    load(norm_b[:, n:n + 1], column(va[P:D]))
                load(w_o1[:, :, :], wo1.rearrange("(c p) n -> p c n", p=P))
                for dst_, src_ in ((w_o2, w_proj2), (w_o3, w_proj3)):
                    load(dst_[:, 0, :], src_[0:P])
                    load(dst_[0:DB, 1, :], src_[P:D])
                load(q_bias1[:, :], bq1.rearrange("(c p) -> p c", p=P))
                load(k_bias1[:, :], bk1.rearrange("(c p) -> p c", p=P))
                load(bv_cols1[:, :], bv1.rearrange("(c p) -> p c", p=P))
                load(bv_cols3[:, 0:1], column(b_qkv3[2 * D:2 * D + P]))
                load(bv_cols3[0:DB, 1:2], column(b_qkv3[2 * D + P:3 * D]))
                for n, t in enumerate((q_bias3, k_bias3)):
                    v = b_qkv3[n * D:(n + 1) * D].rearrange("(c j e) -> j e c", j=4, e=16)
                    for j in range(4):
                        load(t[32 * j:32 * j + 16, :], v[j])
                load(out_bias1[:, :], rows(bo1, TILE))
                load(out_bias2[:, :], rows(b_proj2, TILE))
                load(out_bias3[:, :], rows(b_proj3, TILE))
                load(b_up2[:, :], b_fc1.rearrange("(c p) -> p c", p=P))
                load(w_dn2[:, :, :], w_fc2.rearrange("(c p) n -> p c n", p=P))
                load(b_dn2[:, :], rows(b_fc2, P))

                def scalar_loads(act):
                    act.wait_ge(S["pads_cleared"], PADS + 2)
                    with nc.allow_non_contiguous_dma(reason="bias columns"):
                        for dst_, src_ in loads:
                            act.dma_start(dst_, src_).then_inc(S["small_loaded"], 16)

                def gpsimd(pool):
                    for w in (w_q2, w_k2, w_q3, w_k3):
                        for t in (w.a_hi, w.a_lo, w.b_hi, w.b_lo):
                            nc.gpsimd.memset(t[:, :].bitcast(F32), 0.0).then_inc(S["pads_cleared"], 1)
                    for t in (q_bias3, k_bias3):
                        nc.gpsimd.memset(t[:, :], 0.0).then_inc(S["pads_cleared"], 1)
                    nc.gpsimd.memset(ident[:, :], 0.0).then_inc(S["const_ready"], 1)
                    nc.gpsimd.memset(neg_half[:, :], -0.5)
                    nc.gpsimd.memset(bias1[:, :, :], 0.0).then_inc(S["const_ready"], 1)
                    nc.gpsimd.memset(bias2[:, :, :], 0.0).then_inc(S["const_ready"], 1)
                    nc.gpsimd.iota(distance[:, :], pattern=[[1, UNIT]], base=0, channel_multiplier=-1,
                                   allow_small_or_imprecise_dtypes=True).then_inc(S["const_ready"], 1)
                    nc.gpsimd.iota(iota8[:, :], pattern=[[1, EXPERTS]], base=0, channel_multiplier=0,
                                   allow_small_or_imprecise_dtypes=True)
                    pool.wait_ge(S["const_ready"], 4)
                    nc.gpsimd.affine_select(out=ident[:, :], in_=ident[:, :], compare_op=ALU.not_equal,
                                            fill=1.0, base=0, pattern=[[-1, P]], channel_multiplier=1
                                            ).then_inc(S["const_ready"], 1)
                    nc.gpsimd.affine_select(out=bias1[:, :, :], in_=bias1[:, :, :], compare_op=ALU.is_ge,
                                            fill=NEG, base=0, pattern=[[0, HEADS], [-1, UNIT]],
                                            channel_multiplier=1).then_inc(S["bias1_causal"], 1)
                    nc.gpsimd.tensor_scalar(distance_neg[:, :], distance[:, :], -1.0, None, ALU.mult
                                            ).then_inc(S["const_ready"], 1)
                    pool.wait_ge(S["const_ready"], 6)
                    pool.wait_ge(S["bias1_causal"], 1)
                    pool.wait_ge(S["slopes_applied"], 1)
                    for t in (bias1, bias2, bias3):
                        first, second = t[:, :, 0:SEQ], t[:, :, SEQ:UNIT]
                        nc.gpsimd.affine_select(out=first, in_=first, compare_op=ALU.is_ge, fill=NEG,
                                                base=SEQ - 1, pattern=[[0, HEADS], [0, SEQ]],
                                                channel_multiplier=-1).then_inc(S["bias_ready"], 1)
                        nc.gpsimd.affine_select(out=second, in_=second, compare_op=ALU.is_ge, fill=NEG,
                                                base=-SEQ, pattern=[[0, HEADS], [0, SEQ]],
                                                channel_multiplier=1).then_inc(S["bias_ready"], 1)

                def tensor(pe):
                    pe.wait_ge(S["small_loaded"], 16 * len(loads))
                    for c in range(6):
                        last = nc.tensor.matmul(psum[0:TILE, 3 * BANK:3 * BANK + D],
                                                bv_cols1[:, c:c + 1].to_broadcast([P, TILE]), w_o1[:, c, :],
                                                start=(c == 0), stop=(c == 5))
                    last.then_inc(S["value_bias_done"], 1)
                    for c, p in ((0, P), (1, DB)):
                        last = nc.tensor.matmul(psum[0:TILE, 4 * BANK:4 * BANK + D],
                                                bv_cols3[0:p, c:c + 1].to_broadcast([p, TILE]),
                                                w_o3[0:p, c, :], start=(c == 0), stop=(c == 1))
                    last.then_inc(S["value_bias_done"], 1)

                def vector(dve):
                    dve.wait_ge(S["const_ready"], 6)
                    nc.vector.tensor_tensor(distance[:, :], distance[:, :], distance_neg[:, :], ALU.max
                                            ).then_inc(S["distance_ready"], 1)
                    dve.wait_ge(S["distance_ready"], 1)
                    for n, hh in enumerate(slot_heads(32)):
                        slope = float(np.float32(2.0 ** (-8.0 / HEADS)) ** np.float32(hh + 1))
                        last = nc.vector.tensor_scalar(bias3[:, n, :], distance[:, :], -slope, None,
                                                       ALU.mult)
                    last.then_inc(S["slopes_applied"], 1)
                    dve.wait_ge(S["small_loaded"], 16 * len(loads))
                    nc.vector.tensor_scalar(q_bias1[:, :], q_bias1[:, :], 1.0 / 8, None, ALU.mult)
                    nc.vector.tensor_scalar(q_bias3[:, :], q_bias3[:, :], 1.0 / 4, None, ALU.mult)
                    S_w = S["small_weights"]
                    n = 0

                    def inc(ins):
                        ins.then_inc(S_w, 1)

                    inc(nc.vector.tensor_scalar(w_o2s[:, 0, :], w_o2[:, 0, :], g[:, 0:1], None, ALU.mult))
                    inc(nc.vector.tensor_scalar(w_o2s[0:DB, 1, :], w_o2[0:DB, 1, :], g[0:DB, 0:1], None,
                                                ALU.mult))
                    inc(nc.vector.tensor_scalar(out_bias2s[:, :], out_bias2[:, :], g[0:TILE, 0:1], None,
                                                ALU.mult))
                    inc(nc.vector.tensor_scalar(b_dn2s[:, :], b_dn2[:, :], g[:, 0:1], None, ALU.mult))
                    n = 4
                    for i, kept in ((1, D // 2), (2, D // 3)):
                        dve.wait_ge(S_w, n)
                        for full, part, p in ((w_o2[:, 0, :], w_o2s[:, 0, :], kept),
                                              (out_bias2[:, :], out_bias2s[:, :], TILE),
                                              (b_dn2[:, :], b_dn2s[:, :], P)):
                            inc(nc.vector.scalar_tensor_tensor(
                                out=part[0:p, 0:kept], in0=full[0:p, 0:kept], scalar=g[0:p, i:i + 1],
                                in1=part[0:p, 0:kept], op0=ALU.mult, op1=ALU.add))
                            n += 1
                    for i in range(3):
                        nc.vector.tensor_scalar(w_dn2s[i][:, :, :], w_dn2[:, :, 0:D // (i + 1)],
                                                g[:, i:i + 1], None, ALU.mult)
                    for t, b in ((out_bias1, 3), (out_bias3, 4)):
                        dve.wait_ge(S["value_bias_done"], b - 2)
                        nc.vector.tensor_tensor(t[:, :], psum[0:TILE, b * BANK:b * BANK + D], t[:, :],
                                                ALU.add)

                return {"sync": lambda e: None, "tensor": tensor, "vector": vector, "scalar": lambda e: None,
                        "scalar_loads": scalar_loads, "gpsimd": gpsimd}

            embed_stage(nc, psum, "embed", lambda i: x.rearrange("(c p) (i t) -> i p c t", p=P, t=WIDE)[i],
                        w_tok, tok_w.rearrange("(c p) n -> p c n", p=P), pos, rows(tok_b, TILE),
                        tiles(h[0], TILE), jobs, prepare)
            attention_stage(nc, psum, ident, neg_half, "attn1", tiles(h[0], TILE), tiles(h[1], TILE),
                            TOK // WIDE, 64, 64, w_q1, w_k1, w_v1, w_o1, bias1, q_bias1, k_bias1, 1 / 8,
                            out_bias1[:, :], None, True)

            def norm_cols(n):
                return (norm_a[:, n:n + 1], norm_b[:, n:n + 1], norm_a[:, n + 1:n + 2],
                        norm_b[:, n + 1:n + 2])

            half_a, half_m = TOK // WIDE // 2, TOK // MW // 2
            for part, w_o, o_bias, cols in ((0, w_o2, out_bias2, 0), (1, w_o2s, out_bias2s, 2)):
                attention_stage(nc, psum, ident, neg_half, f"attn2{part}",
                                tiles(h[1], TILE, part * half_a), tiles(x1, TILE, part * half_a),
                                half_a, 16, 32, w_q2, w_k2, w_v2, w_o, bias2, None, None, 1 / 4,
                                o_bias[:, :], norm_cols(cols), False)
            kept = [(D // (n + 1), w_dn2s[n]) for n in range(3)]
            for part, branches, o_bias, cols in ((0, [(D, w_dn2)], b_dn2, 4), (1, kept, b_dn2s, 6)):
                mlp_stage(nc, psum, ident, neg_half, f"mlp{part}", tiles(h[1], MT, part * half_m),
                          tiles(x1, MT, part * half_m), tiles(h[2], MT, part * half_m), half_m, w_up2,
                          b_up2, branches, o_bias[:, :], norm_cols(cols))

        w_gu = Split(sb, "w_gu", 2 * HID + 2 * EH)
        w_dn_shared, w_dn = sb("w_dn_shared", [P, 6, D]), sb("w_dn", [P, EH // P, D])
        w_dn_mid = sb("w_dn_mid", [P, EXPERTS, D])
        side = MoeWeights(nc, top, sb, w_gu, w_gu_dram, w_dn_shared, ws_down, w_dn, w_down, w_dn_mid)
        attention_stage(nc, psum, ident, neg_half, "attn3", tiles(h[2], TILE), tiles(h[3], TILE),
                        TOK // WIDE, 16, 32, w_q3, w_k3, w_v3, w_o3, bias3, q_bias3, k_bias3, 1 / 4,
                        out_bias3[:, :], None, True, side)
        moe_stage(nc, psum, ident, neg_half, "moe", tiles(h[3], MT), tiles(out, MT), TOK // MW, w_gu,
                  w_router, sg_bias[:, :], w_dn_shared, w_dn, w_dn_mid, iota8[:, :])


def kernel(x, L0_tok_W_proj, L0_tok_b_proj, L0_tok_pos_table, L0_attn_W_Q, L0_attn_b_Q, L0_attn_W_K,
           L0_attn_b_K, L0_attn_W_V, L0_attn_b_V, L0_attn_W_O, L0_attn_b_O, L0_ffn_gumbel_weights,
           L0_ffn_n1l_g, L0_ffn_n1l_b, L0_ffn_n1s_g, L0_ffn_n1s_b, L0_ffn_w_qkv, L0_ffn_w_proj,
           L0_ffn_b_proj, L0_ffn_n2l_g, L0_ffn_n2l_b, L0_ffn_n2s_g, L0_ffn_n2s_b, L0_ffn_w_fc1,
           L0_ffn_b_fc1, L0_ffn_w_fc2, L0_ffn_b_fc2, L1_attn_w_qkv, L1_attn_b_qkv, L1_attn_w_proj,
           L1_attn_b_proj, L1_ffn_router_w, L1_ffn_w_gate, L1_ffn_w_up, L1_ffn_w_down, L1_ffn_ws_gate,
           L1_ffn_ws_up, L1_ffn_ws_down, L1_ffn_sg_w, L1_ffn_sg_b):
    import concourse.bacc as _bacc
    from concourse.bass_utils import run_bass_kernel_spmd as _run

    def flat(w):
        return np.asarray(w).transpose(1, 0, 2).reshape(D, -1)

    g = SIDE // PATCH
    patches = np.asarray(x).reshape(IMAGES, g, PATCH, g, PATCH, 3).transpose(2, 4, 5, 0, 1, 3)
    host = {
        "x": patches.reshape(PATCH_K, TOK),
        "tok_w": L0_tok_W_proj, "tok_b": L0_tok_b_proj,
        "pos": np.tile(np.asarray(L0_tok_pos_table), (WIDE // SEQ, 1)).reshape(TILES, TILE, D)
                 .transpose(1, 0, 2),
        "wq1": flat(L0_attn_W_Q), "bq1": np.asarray(L0_attn_b_Q).reshape(-1),
        "wk1": flat(L0_attn_W_K), "bk1": np.asarray(L0_attn_b_K).reshape(-1),
        "wv1": flat(L0_attn_W_V), "bv1": np.asarray(L0_attn_b_V).reshape(-1),
        "wo1": np.asarray(L0_attn_W_O).reshape(HID, D), "bo1": L0_attn_b_O,
        "gumbel": L0_ffn_gumbel_weights,
        "n1l_g": L0_ffn_n1l_g, "n1l_b": L0_ffn_n1l_b, "n1s_g": L0_ffn_n1s_g, "n1s_b": L0_ffn_n1s_b,
        "w_qkv2": L0_ffn_w_qkv, "w_proj2": L0_ffn_w_proj, "b_proj2": L0_ffn_b_proj,
        "n2l_g": L0_ffn_n2l_g, "n2l_b": L0_ffn_n2l_b, "n2s_g": L0_ffn_n2s_g, "n2s_b": L0_ffn_n2s_b,
        "w_fc1": L0_ffn_w_fc1, "b_fc1": L0_ffn_b_fc1, "w_fc2": L0_ffn_w_fc2, "b_fc2": L0_ffn_b_fc2,
        "w_qkv3": np.asarray(L1_attn_w_qkv).T, "b_qkv3": L1_attn_b_qkv,
        "w_proj3": np.asarray(L1_attn_w_proj).T, "b_proj3": L1_attn_b_proj,
        "w_gu_dram": np.concatenate([np.asarray(L1_ffn_ws_gate), np.asarray(L1_ffn_ws_up),
                                     flat(L1_ffn_w_gate), flat(L1_ffn_w_up)], axis=1),
        "w_router_dram": np.concatenate([np.asarray(L1_ffn_router_w)] + 2 * [np.asarray(L1_ffn_sg_w)],
                                        axis=1),
        "w_down": np.asarray(L1_ffn_w_down).reshape(EH, D), "ws_down": L1_ffn_ws_down,
        "sg_b": L1_ffn_sg_b,
    }
    nc = _bacc.Bacc("TRN2", target_bir_lowering=False, num_devices=1)
    arrays, args = {}, {}
    for name, value in host.items():
        a = np.ascontiguousarray(value)
        arrays["in_" + name] = a
        args[name] = nc.dram_tensor("in_" + name, a.shape, mybir.dt.from_np(a.dtype),
                                    kind="ExternalInput").ap()
    args["out"] = nc.dram_tensor("y", [TOK, D], F32, kind="ExternalOutput").ap()
    build(nc, **args)
    r = _run(nc, [arrays], core_ids=[0])
    return r.results[0]["y"].reshape(IMAGES, SEQ, D)
```

```python
from contextlib import ExitStack

import numpy as np

import concourse.bass as bass
import concourse.mybir as mybir

F32 = mybir.dt.float32
F32R = mybir.dt.float32r
U32 = mybir.dt.uint32
ALU = mybir.AluOpType
ACT = mybir.ActivationFunctionType
AX = mybir.AxisListType

P = 128
IMAGES, SIDE, PATCH = 64, 96, 16
SEQ = (SIDE // PATCH) ** 2
TOK = IMAGES * SEQ
D = 192
DB = D - P
PATCH_K = PATCH * PATCH * 3
HEADS = 12
HID = 768
EXPERTS = 8
EH = EXPERTS * D
EPS = 1e-5
NEG = -1e30

UNIT = 2 * SEQ
UNITS = 4
TILE = 96
TILES = 3
WIDE = UNITS * UNIT
HB = HEADS // 2
MT = 128
MW = 3 * MT
BANK = 512


class Split:

    def __init__(self, sb, name, n):
        self.n = n
        self.a_hi = sb(name + "_a_hi", [P, n], F32R)
        self.a_lo = sb(name + "_a_lo", [P, n], F32R)
        self.b_hi = sb(name + "_b_hi", [P, n], F32R)
        self.b_lo = sb(name + "_b_lo", [DB, n], F32R)


class SplitX:

    def __init__(self, sb, name, n):
        self.a_hi = sb(name + "_a_hi", [P, n], F32R)
        self.a_lo = sb(name + "_a_lo", [P, n], F32R)
        self.b = sb(name + "_b", [P, n], F32R)


def weight_by_x(nc, out, w, cols, x, toks):
    nc.tensor.matmul(out, w.a_hi[:, cols], x.a_hi[:, toks], start=True, stop=False)
    nc.tensor.matmul(out, w.a_hi[:, cols], x.a_lo[:, toks], start=False, stop=False)
    nc.tensor.matmul(out, w.a_lo[:, cols], x.a_hi[:, toks], start=False, stop=False)
    nc.tensor.matmul(out, w.b_hi[:, cols], x.b[:, toks], start=False, stop=False)
    return nc.tensor.matmul(out, w.b_lo[:, cols], x.b[0:DB, toks], start=False, stop=True)


def weight_by_x_head(nc, out, w, cols, x, toks, k):
    nc.tensor.matmul(out, w.a_hi[0:k, cols], x.a_hi[0:k, toks], start=True, stop=False)
    nc.tensor.matmul(out, w.a_hi[0:k, cols], x.a_lo[0:k, toks], start=False, stop=False)
    return nc.tensor.matmul(out, w.a_lo[0:k, cols], x.a_hi[0:k, toks], start=False, stop=True)


def x_by_weight(nc, out, x, toks, w, cols):
    nc.tensor.matmul(out, x.a_hi[:, toks], w.a_hi[:, cols], start=True, stop=False)
    nc.tensor.matmul(out, x.a_lo[:, toks], w.a_hi[:, cols], start=False, stop=False)
    nc.tensor.matmul(out, x.a_hi[:, toks], w.a_lo[:, cols], start=False, stop=False)
    nc.tensor.matmul(out, x.b[:, toks], w.b_hi[:, cols], start=False, stop=False)
    return nc.tensor.matmul(out, x.b[0:DB, toks], w.b_lo[:, cols], start=False, stop=True)


def column(v):
    return v.rearrange("(p a) -> p a", a=1)


def rows(v, p):
    return v.rearrange("(a n) -> a n", a=1).to_broadcast([p, v.shape[0]])


def wait_apart(eng, sem, value):
    eng.wait_ge(sem, value)
    eng.nop(nofuse=True)


class Sems:

    def __init__(self, nc, prefix):
        self._nc, self._prefix, self._made = nc, prefix, {}

    def __enter__(self):
        return self

    def __exit__(self, *_):
        self._nc.clear_and_free_semaphores(list(self._made.values()))
        self._nc.all_engine_barrier()

    def __getitem__(self, name):
        if name not in self._made:
            self._made[name] = self._nc.alloc_semaphore(name=f"{self._prefix}_{name}")
        return self._made[name]



def attention_stage(nc, psum, ident, neg_half, name, src, dst, n_iter, dh, hb_rows, w_q, w_k, w_v,
                    bias_hk, q_bias, k_bias, q_scale, parts, postnorm, side=None):
    share = n_iter // len(parts)
    prenorm = parts[0][2] is not None
    heads_per_chunk = P // hb_rows
    chunks = HEADS // heads_per_chunk
    v_banks = 2 if dh == 64 else 1
    v_cols = HEADS * dh // v_banks

    with Sems(nc, name) as S, ExitStack() as ctx:
        def sb(nm, shape, dt=F32):
            return ctx.enter_context(nc.sbuf_tensor(f"{name}_{nm}", shape, dt))

        x_tok = sb("x_tok", [TILE, TILES, D])
        res_tok = sb("res_tok", [TILE, TILES, D])
        residual = sb("residual", [TILE, TILES, D])
        y = sb("y", [TILE, TILES, D])
        xs = SplitX(sb, "x", WIDE)
        q = [sb(f"q{c}", [P, WIDE]) for c in range(chunks)]
        k_diag = sb("k_diag", [P, chunks, UNITS, heads_per_chunk, UNIT])
        v = [sb(f"v{s}", [UNIT, HEADS, hb_rows]) for s in range(UNITS)]
        prob = [sb(f"prob{s}", [UNIT, HEADS, UNIT]) for s in range(UNITS)]
        row_max = [sb(f"row_max{s}", [UNIT, HEADS]) for s in range(UNITS)]
        prob_t = sb("prob_t", [UNIT, HEADS, UNIT])
        row_sum = sb("row_sum", [UNIT, HEADS])
        sum_recip = [sb(f"sum_recip{p}", [UNIT, HEADS]) for p in range(2)]
        recip_wide = [sb(f"recip_wide{p}", [UNIT, HEADS, hb_rows]) for p in range(2)]
        recip_t = sb("recip_t", [P, chunks, UNIT])
        z_t = sb("z_t", [P, chunks, WIDE])
        stats = sb("stats", [TILE, TILES, 6])
        mean_var = sb("mean_var", [TILE, TILES, 2])
        var_eps = sb("var_eps", [TILE, TILES])
        rstd = sb("rstd", [TILE, TILES])
        if prenorm:
            x_hat = sb("x_hat", [TILE, TILES, D])
            x_aff_a, x_aff_b = sb("x_aff_a", [P, WIDE]), sb("x_aff_b", [DB, WIDE])
            pre_stats = sb("pre_stats", [TILE, TILES, 6])
            pre_mv = sb("pre_mv", [TILE, TILES, 2])
            pre_var = sb("pre_var", [TILE, TILES])
            pre_rstd = sb("pre_rstd", [TILE, TILES])

        def bank(b):
            return psum[:, b * BANK:(b + 1) * BANK]

        def scores_bank(b, p=UNIT):
            return bank(b)[0:p, 0:HB * UNIT].rearrange("p (h k) -> p h k", h=HB)

        z_ps, recip_ps = (bank(b)[:, 0:chunks * UNIT].rearrange("p (c t) -> p c t", t=UNIT) for b in (6, 7))

        def out_bank(t):
            return bank(7 if t == 1 else 6)[0:TILE, 0:D]

        last_q = (chunks - 1) % 2
        qk_bank = [c % 2 for c in range(chunks)] + [(1 - last_q, 7, last_q)[n % 3] for n in range(chunks)]
        before = [max((d for d in range(c) if qk_bank[d] == qk_bank[c]), default=None)
                  for c in range(2 * chunks)]

        block = ctx.enter_context(nc.Block())

        @block.sync
        def _(sp):
            def load_x(i):
                sp.wait_ge(S["x_hat_ready" if prenorm else "x_transposed"], i)
                sp.dma_start(x_tok[:, :, :], src(i)).then_inc(S["x_loaded"], 16)

            def load_residual(i):
                sp.wait_ge(S["residual_ready"], i)
                sp.dma_start(res_tok[:, :, :], src(i)).then_inc(S["res_loaded"], 16)

            def store(i):
                sp.wait_ge(S["y_ready" if postnorm else "attn_added"], TILES * i + TILES)
                sp.dma_start(dst(i), y[:, :, :]).then_inc(S["y_stored"], 16)

            sp.dma_start(x_tok[:, :, :], src(0)).then_inc(S["x_loaded"], 16)
            sp.dma_start(res_tok[:, :, :], src(0)).then_inc(S["res_loaded"], 16)
            load_x(1)
            if side:
                side.load_start(sp)

            def step(i):
                if side:
                    side.load_step(sp, i)
                if not isinstance(i, int) or i < n_iter - 2:
                    load_x(i + 2)
                if not isinstance(i, int) or i < n_iter - 1:
                    load_residual(i + 1)
                store(i)

            with sp.Fori(0, n_iter - 2) as i:
                step(i)
            step(n_iter - 2)
            step(n_iter - 1)
            sp.wait_ge(S["y_stored"], 16 * n_iter)

        @block.gpsimd
        def _(pool):
            nc.gpsimd.memset(k_diag[:, :, :, :, :].rearrange("p c s j t -> p (c s j t)"), 0.0
                             ).then_inc(S["keys_cleared"], 1)
            if dh < hb_rows:
                for s in range(UNITS):
                    nc.gpsimd.memset(v[s][:, :, dh:hb_rows], 1.0).then_inc(S["values_padded"], 1)

            def shift(i, s):
                for b in range(2):
                    pool.wait_ge(S["max_done"], 2 * (UNITS * i + s) + b + 1)
                    hs = slice(b * HB, (b + 1) * HB)
                    nc.gpsimd.tensor_tensor(prob[s][:, hs, :], prob[s][:, hs, :],
                                            row_max[s][:, hs].rearrange("p (h a) -> p h a", a=1)
                                            .to_broadcast([UNIT, HB, UNIT]), ALU.subtract
                                            ).then_inc(S["shifted"], 1)

            def make_residual(i, part):
                out_bias = parts[part][1]
                pool.wait_ge(S["res_loaded"], 16 * i + 16)
                pool.wait_ge(S["attn_added"], TILES * i)
                nc.gpsimd.tensor_tensor(residual[:, :, :], res_tok[:, :, :],
                                        out_bias.rearrange("p (a n) -> p a n", a=1)
                                        .to_broadcast([TILE, TILES, D]), ALU.add
                                        ).then_inc(S["residual_ready"], 1)

            def pre_pow(i):
                pool.wait_ge(S["pre_var_ready"], i + 1)
                nc.gpsimd.tensor_tensor(pre_rstd[:, :], pre_var[:, :],
                                        neg_half[0:TILE, 0:TILES], ALU.pow
                                        ).then_inc(S["pre_rstd_ready"], 1)

            def out_pow(i, t):
                if postnorm:
                    pool.wait_ge(S["var_ready"], TILES * i + t + 1)
                    nc.gpsimd.tensor_tensor(rstd[:, t:t + 1], var_eps[:, t:t + 1],
                                            neg_half[0:TILE, 0:1], ALU.pow).then_inc(S["rstd_ready"], 1)

            def body(i, part, last, ahead):
                shift(i, 2)
                make_residual(i, part)
                shift(i, 3)
                if prenorm and ahead:
                    pre_pow(i + 2)
                if side:
                    side.split_step(pool, i)
                if not last:
                    shift(i + 1, 0)
                    shift(i + 1, 1)
                for t in range(TILES):
                    out_pow(i, t)

            if prenorm:
                pre_pow(0)
                pre_pow(1)
            if side:
                side.split_start(pool)
            shift(0, 0)
            shift(0, 1)
            for part in range(len(parts)):
                end = (part + 1) * share
                with pool.Fori(part * share, end - 2 * (end == n_iter)) as i:
                    body(i, part, False, True)
            body(n_iter - 2, part, False, False)
            body(n_iter - 1, part, True, False)

        @block.tensor
        def _(pe):
            def transpose_x(i):
                pe.wait_ge(S["x_loaded"], 16 * i + 16)
                if prenorm:
                    pe.wait_ge(S["x_hat_ready"], i + 1)
                pe.wait_ge(S["v_evacuated"], UNITS * i)
                tok = x_hat if prenorm else x_tok
                for t in range(TILES):
                    nc.tensor.transpose(bank(0)[:, t * TILE:(t + 1) * TILE], tok[:, t, 0:P],
                                        ident[0:TILE, 0:TILE])
                    last = nc.tensor.transpose(bank(1)[0:DB, t * TILE:(t + 1) * TILE], tok[:, t, P:D],
                                               ident[0:TILE, 0:TILE])
                last.then_inc(S["x_transposed"], 1)

            def project_qk(i, c0, c1):
                for c in range(c0, c1):
                    if c == 0:
                        pe.wait_ge(S["x_split"], i + 1)
                    elif before[c] is not None:
                        pe.wait_ge(S["qk_evacuated"], 2 * chunks * i + before[c] + 1)
                        if before[c] >= chunks:
                            pe.wait_ge(S["k_half_evacuated"], chunks * i + before[c] + 1 - chunks)
                    elif qk_bank[c] == 7 and not (isinstance(i, int) and i == 0):
                        pe.wait_ge(S["recip_copied"], UNITS * i - 1)
                    w = w_q if c < chunks else w_k
                    at = (c % chunks) * P
                    weight_by_x(nc, bank(qk_bank[c])[:, 0:WIDE], w, slice(at, at + P), xs, slice(0, WIDE)
                                ).then_inc(S["qk_done"], 1)

            def scores(i, s):
                if s == 0:
                    pe.wait_ge(S["qk_evacuated"], 2 * chunks * (i + 1))
                    pe.wait_ge(S["k_half_evacuated"], chunks * (i + 1))
                toks = slice(s * UNIT, (s + 1) * UNIT)
                pe.wait_ge(S["scores_biased"], 2 * (UNITS * i + s))
                for b in range(2):
                    for c in range(chunks):
                        h0 = max(c * heads_per_chunk, b * HB)
                        h1 = min((c + 1) * heads_per_chunk, (b + 1) * HB)
                        if h0 < h1:
                            j0, j1 = h0 - c * heads_per_chunk, h1 - c * heads_per_chunk
                            last = nc.tensor.matmul(scores_bank(2 + b)[:, h0 - b * HB:h1 - b * HB, :],
                                                    q[c][:, toks], k_diag[:, c, s, j0:j1, :],
                                                    start=True, stop=True)
                    last.then_inc(S["scores_done"], 1)

            def values(i, s):
                pe.wait_ge(S["v_evacuated"], UNITS * i + s)
                toks = slice(s * UNIT, (s + 1) * UNIT)
                for b in range(v_banks):
                    last = x_by_weight(nc, bank(b)[0:UNIT, 0:v_cols], xs, toks, w_v,
                                       slice(b * v_cols, (b + 1) * v_cols))
                last.then_inc(S["v_done"], 1)

            def transpose_prob(i, s):
                for b in range(2):
                    pe.wait_ge(S["exp_done"], 2 * (UNITS * i + s) + b + 1)
                    for hh in range(HB):
                        last = nc.tensor.transpose(scores_bank(4 + b)[:, hh, :],
                                                   prob[s][:, b * HB + hh, :], ident[0:UNIT, 0:UNIT])
                    last.then_inc(S["prob_transposed"], 1)

            def mix_values(i, s):
                pe.wait_ge(S["v_evacuated"], UNITS * i + s + 1)
                pe.wait_ge(S["z_normalised"], UNITS * i + s)
                if s == 0:
                    pe.wait_ge(S["attn_added"], TILES * i)
                elif s == 3:
                    pe.wait_ge(S["attn_added"], TILES * i + 1)
                for h in range(HEADS):
                    if h % HB == 0:
                        pe.wait_ge(S["prob_t_evacuated"], 2 * (UNITS * i + s) + h // HB + 1)
                    c, r = h // heads_per_chunk, (h % heads_per_chunk) * hb_rows
                    last = nc.tensor.matmul(z_ps[r:r + hb_rows, c, :], v[s][:, h, :], prob_t[:, h, :],
                                            start=True, stop=True)
                last.then_inc(S["values_mixed"], 1)

            def turn_recip(i, s):
                pe.wait_ge(S["recip_spread"], UNITS * i + s + 1)
                pe.wait_ge(S["recip_copied"], UNITS * i + s)
                flat = recip_wide[s % 2][:, :, :].rearrange("p h r -> p (h r)")
                for c in range(chunks):
                    last = nc.tensor.matmul(recip_ps[:, c, :], flat[:, c * P:(c + 1) * P],
                                            ident[0:UNIT, 0:UNIT], start=True, stop=True)
                last.then_inc(S["recip_turned"], 1)

            def project_out(i, t, part):
                w_o = parts[part][0]
                pe.wait_ge(S["z_normalised"], UNITS * i + (4 if t == 2 else 3))
                if t == 1:
                    pe.wait_ge(S["recip_copied"], UNITS * i + 4)
                for c in range(chunks):
                    last = nc.tensor.matmul(out_bank(t), z_t[:, c, t * TILE:(t + 1) * TILE], w_o[:, c, :],
                                            start=(c == 0), stop=(c == chunks - 1))
                last.then_inc(S["out_done"], 1)

            def body(i, part, last):
                for s in range(2):
                    scores(i, s + 2)
                    transpose_prob(i, s)
                    values(i, s + 2)
                    mix_values(i, s)
                    if s == 1 and not last:
                        transpose_x(i + 1)
                    turn_recip(i, s)
                transpose_prob(i, 2)
                if not last:
                    project_qk(i + 1, 0, chunks)
                mix_values(i, 2)
                turn_recip(i, 2)
                if not last:
                    project_qk(i + 1, chunks, 2 * chunks)
                project_out(i, 0, part)
                transpose_prob(i, 3)
                if not last:
                    scores(i + 1, 0)
                    values(i + 1, 0)
                mix_values(i, 3)
                turn_recip(i, 3)
                if not last:
                    scores(i + 1, 1)
                project_out(i, 1, part)
                if not last:
                    values(i + 1, 1)
                project_out(i, 2, part)

            if dh < hb_rows:
                pe.wait_ge(S["values_padded"], UNITS)
            transpose_x(0)
            project_qk(0, 0, 2 * chunks)
            for s in range(2):
                scores(0, s)
                values(0, s)
            for part in range(len(parts)):
                end = (part + 1) * share
                last = end == n_iter
                with pe.Fori(part * share, end - last) as i:
                    body(i, part, False)
            body(n_iter - 1, part, True)

        @block.scalar
        def _(act):
            def round_x(i, part):
                act.wait_ge(S["x_transposed"], i + 1)
                if prenorm:
                    ga, gb, ba, bb = parts[part][2]
                    nc.scalar.activation(x_aff_a[:, :], bank(0)[:, 0:WIDE], ACT.Identity, bias=ba, scale=ga
                                         ).then_inc(S["x_affine"], 1)
                    nc.scalar.activation(x_aff_b[:, :], bank(1)[0:DB, 0:WIDE], ACT.Identity, bias=bb,
                                         scale=gb).then_inc(S["x_affine"], 1)
                    act.wait_ge(S["x_affine"], 2 * i + 2)
                    nc.scalar.activation(xs.a_hi[:, :], x_aff_a[:, :], ACT.Copy).then_inc(S["x_rounded"], 1)
                    nc.scalar.activation(xs.b[0:DB, :], x_aff_b[:, :], ACT.Copy).then_inc(S["x_rounded"], 1)
                else:
                    nc.scalar.activation(xs.a_hi[:, :], bank(0)[:, 0:WIDE], ACT.Copy
                                         ).then_inc(S["x_rounded"], 1)
                    nc.scalar.activation(xs.b[0:DB, :], bank(1)[0:DB, 0:WIDE], ACT.Copy
                                         ).then_inc(S["x_rounded"], 1)

            def copy_chunk(out, rows_, b, bias, n, scale):
                in_ = bank(b)[rows_, 0:WIDE]
                if len(out.shape) == 3:
                    in_ = in_.rearrange("p (s t) -> p s t", s=UNITS)
                if bias is None:
                    return nc.scalar.activation(out, in_, ACT.Copy, scale=scale)
                return nc.scalar.activation(out, in_, ACT.Identity, bias=bias[rows_, n:n + 1], scale=scale)

            def copy_qk(i, c0, c1):
                for c in range(c0, c1):
                    act.wait_ge(S["qk_done"], 2 * chunks * i + c + 1)
                    if c < chunks:
                        ins = copy_chunk(q[c][:, :], slice(0, P), qk_bank[c], q_bias, c, q_scale)
                    else:
                        n = c - chunks
                        for j in range(heads_per_chunk // 2):
                            rows_ = slice(j * hb_rows, (j + 1) * hb_rows)
                            ins = copy_chunk(k_diag[rows_, n, :, j, :], rows_, qk_bank[c], k_bias, n, 1.0)
                    ins.then_inc(S["qk_evacuated"], 1)

            def copy_v(i, s):
                act.wait_ge(S["v_done"], UNITS * i + s + 1)
                src_ = psum[0:UNIT, 0:v_banks * BANK].rearrange("p (b n) -> p b n", b=v_banks)[
                    :, :, 0:v_cols].rearrange("p b (h e) -> p b h e", e=dh)
                out = v[s][:, :, :].rearrange("p (b h) e -> p b h e", b=v_banks)[:, :, :, 0:dh]
                nc.scalar.activation(out, src_, ACT.Copy).then_inc(S["v_evacuated"], 1)

            def exponentiate(i, s):
                for b in range(2):
                    act.wait_ge(S["shifted"], 2 * (UNITS * i + s) + b + 1)
                    part = prob[s][:, b * HB:(b + 1) * HB, :]
                    nc.scalar.activation(part, part, ACT.Exp).then_inc(S["exp_done"], 1)

            def copy_prob_t(i, s):
                for b in range(2):
                    act.wait_ge(S["prob_transposed"], 2 * (UNITS * i + s) + b + 1)
                    nc.scalar.activation(prob_t[:, b * HB:(b + 1) * HB, :], scores_bank(4 + b), ACT.Copy
                                         ).then_inc(S["prob_t_evacuated"], 1)

            def spread_recip(i, s):
                act.wait_ge(S["recip_ready"], UNITS * i + s + 1)
                nc.scalar.activation(recip_wide[s % 2][:, :, :],
                                     sum_recip[s % 2][:, :].rearrange("p (h a) -> p h a", a=1)
                                     .to_broadcast([UNIT, HEADS, hb_rows]), ACT.Copy
                                     ).then_inc(S["recip_spread"], 1)

            def copy_recip(i, s):
                act.wait_ge(S["recip_turned"], UNITS * i + s + 1)
                act.wait_ge(S["z_normalised"], UNITS * i + s)
                nc.scalar.activation(recip_t[:, :, :], recip_ps, ACT.Copy).then_inc(S["recip_copied"], 1)

            def body(i, next_part, last):
                for s in range(2):
                    copy_prob_t(i, s)
                    spread_recip(i, s)
                    copy_v(i, s + 2)
                    exponentiate(i, s + 1)
                    if s == 1 and not last:
                        round_x(i + 1, next_part)
                    copy_recip(i, s)
                copy_prob_t(i, 2)
                if not last:
                    copy_qk(i + 1, 0, chunks)
                spread_recip(i, 2)
                exponentiate(i, 3)
                copy_recip(i, 2)
                if side:
                    side.round_step(act, i)
                if not last:
                    copy_qk(i + 1, chunks, 2 * chunks)
                copy_prob_t(i, 3)
                spread_recip(i, 3)
                if not last:
                    copy_v(i + 1, 0)
                copy_recip(i, 3)
                if not last:
                    exponentiate(i + 1, 0)
                    copy_v(i + 1, 1)

            round_x(0, 0)
            act.wait_ge(S["keys_cleared"], 1)
            copy_qk(0, 0, 2 * chunks)
            copy_v(0, 0)
            copy_v(0, 1)
            exponentiate(0, 0)
            for part in range(len(parts)):
                with act.Fori(max(0, part * share - 1), (part + 1) * share - 1) as i:
                    body(i, part, False)
            body(n_iter - 1, None, True)

        @block.vector
        def _(dve):
            def pre_stat(i):
                dve.wait_ge(S["x_loaded"], 16 * i + 16)
                for t in range(TILES):
                    nc.vector.bn_stats(pre_stats[:, t, :], x_tok[:, t, :]).then_inc(S["pre_stats_ready"], 1)
                for t in range(TILES):
                    wait_apart(dve, S["pre_stats_ready"], TILES * i + t + 1)
                    nc.vector.bn_aggr(pre_mv[:, t, :], pre_stats[:, t, :]).then_inc(S["pre_mv_ready"], 1)
                dve.wait_ge(S["pre_mv_ready"], TILES * (i + 1))
                nc.vector.tensor_scalar(pre_var[:, :], pre_mv[:, :, 1], EPS, None, ALU.add
                                        ).then_inc(S["pre_var_ready"], 1)

            def pre_norm(i):
                dve.wait_ge(S["pre_rstd_ready"], i + 1)
                dve.wait_ge(S["x_transposed"], i)
                for t in range(TILES):
                    last = nc.vector.tensor_scalar(x_hat[:, t, :], x_tok[:, t, :], pre_mv[:, t, 0:1],
                                                   pre_rstd[:, t:t + 1], ALU.subtract, ALU.mult)
                last.then_inc(S["x_hat_ready"], 1)

            def copy_k(i):
                for n in range(chunks):
                    c = chunks + n
                    dve.wait_ge(S["qk_done"], 2 * chunks * i + c + 1)
                    for j in range(heads_per_chunk // 2, heads_per_chunk):
                        rows_ = slice(j * hb_rows, (j + 1) * hb_rows)
                        in_ = bank(qk_bank[c])[rows_, 0:WIDE].rearrange("p (s t) -> p s t", s=UNITS)
                        if k_bias is None:
                            ins = nc.vector.tensor_copy(k_diag[rows_, n, :, j, :], in_)
                        else:
                            ins = nc.vector.tensor_scalar(k_diag[rows_, n, :, j, :], in_,
                                                          k_bias[rows_, n:n + 1], None, ALU.add)
                    ins.then_inc(S["k_half_evacuated"], 1)

            def split_x(i):
                a_ps, b_ps = bank(0)[:, 0:WIDE], bank(1)[0:DB, 0:WIDE]
                dve.wait_ge(S["x_rounded"], 2 * i + 2)
                if prenorm:
                    a_ps, b_ps = x_aff_a[:, :], x_aff_b[:, :]
                nc.vector.tensor_tensor(xs.a_lo[:, :], a_ps, xs.a_hi[:, :].bitcast(F32), ALU.subtract)
                nc.vector.tensor_tensor(xs.b[DB:P, :], b_ps, xs.b[0:DB, :].bitcast(F32), ALU.subtract
                                        ).then_inc(S["x_split"], 1)

            def softmax(i, s):
                u = UNITS * i + s
                pr, mx = prob[s], row_max[s]
                for b in range(2):
                    hs = slice(b * HB, (b + 1) * HB)
                    dve.wait_ge(S["scores_done"], 2 * u + b + 1)
                    nc.vector.tensor_tensor(pr[:, hs, :], scores_bank(2 + b), bias_hk[:, hs, :], ALU.add
                                            ).then_inc(S["scores_biased"], 1)
                for b in range(2):
                    hs = slice(b * HB, (b + 1) * HB)
                    dve.wait_ge(S["scores_biased"], 2 * u + b + 1)
                    nc.vector.tensor_reduce(mx[:, hs], pr[:, hs, :], axis=AX.X, op=ALU.max
                                            ).then_inc(S["max_done"], 1)

            def sum_up(i, s):
                u = UNITS * i + s
                dve.wait_ge(S["exp_done"], 2 * u + 2)
                nc.vector.tensor_reduce(row_sum[:, :], prob[s][:, :, :], axis=AX.X, op=ALU.add
                                        ).then_inc(S["sum_ready"], 1)
                dve.wait_ge(S["sum_ready"], u + 1)
                nc.vector.reciprocal(sum_recip[s % 2][:, :], row_sum[:, :]).then_inc(S["recip_ready"], 1)

            def normalise_z(i, s):
                dve.wait_ge(S["values_mixed"], UNITS * i + s + 1)
                dve.wait_ge(S["recip_copied"], UNITS * i + s + 1)
                nc.vector.tensor_tensor(z_t[:, :, s * UNIT:(s + 1) * UNIT], z_ps, recip_t[:, :, :], ALU.mult
                                        ).then_inc(S["z_normalised"], 1)

            def add_residual(i, t):
                dve.wait_ge(S["out_done"], TILES * i + t + 1)
                dve.wait_ge(S["residual_ready"], i + 1)
                if t == 0:
                    dve.wait_ge(S["y_stored"], 16 * i)
                nc.vector.tensor_tensor(y[:, t, :], out_bank(t), residual[:, t, :], ALU.add
                                        ).then_inc(S["attn_added"], 1)
                if not postnorm:
                    return
                n = TILES * i + t + 1
                dve.wait_ge(S["attn_added"], n)
                nc.vector.bn_stats(stats[:, t, :], y[:, t, :]).then_inc(S["stats_ready"], 1)
                wait_apart(dve, S["stats_ready"], n)
                nc.vector.bn_aggr(mean_var[:, t, :], stats[:, t, :]).then_inc(S["mean_ready"], 1)
                dve.wait_ge(S["mean_ready"], n)
                nc.vector.tensor_scalar(var_eps[:, t:t + 1], mean_var[:, t, 1:2], EPS, None, ALU.add
                                        ).then_inc(S["var_ready"], 1)

            def post_norm(i, t):
                if not postnorm:
                    return
                dve.wait_ge(S["rstd_ready"], TILES * i + t + 1)
                nc.vector.tensor_scalar(y[:, t, :], y[:, t, :], mean_var[:, t, 0:1], rstd[:, t:t + 1],
                                        ALU.subtract, ALU.mult).then_inc(S["y_ready"], 1)

            def body(i, last, ahead):
                softmax(i, 2)
                normalise_z(i, 0)
                sum_up(i, 1)
                softmax(i, 3)
                if not last:
                    split_x(i + 1)
                normalise_z(i, 1)
                sum_up(i, 2)
                if prenorm and ahead:
                    pre_stat(i + 2)
                    pre_norm(i + 2)
                normalise_z(i, 2)
                if not last:
                    copy_k(i + 1)
                sum_up(i, 3)
                add_residual(i, 0)
                if not last:
                    softmax(i + 1, 0)
                normalise_z(i, 3)
                if not last:
                    softmax(i + 1, 1)
                add_residual(i, 1)
                add_residual(i, 2)
                if not last:
                    sum_up(i + 1, 0)
                for t in range(TILES):
                    post_norm(i, t)

            if prenorm:
                pre_stat(0)
                pre_norm(0)
            split_x(0)
            dve.wait_ge(S["keys_cleared"], 1)
            copy_k(0)
            if prenorm:
                pre_stat(1)
                pre_norm(1)
            softmax(0, 0)
            softmax(0, 1)
            sum_up(0, 0)
            with dve.Fori(0, n_iter - 2) as i:
                body(i, False, True)
            body(n_iter - 2, False, False)
            body(n_iter - 1, True, False)



def mlp_stage(nc, psum, ident, neg_half, name, h_src, x_src, dst, n_iter, w_up, b_up, parts):
    chunks = HID // P
    share = n_iter // len(parts)
    per_iter = [chunks * len(branches) for branches, _, _ in parts]

    def before(part, j):
        return share * sum(per_iter[:part]) + per_iter[part] * j

    def over_iterations(eng, body):
        for part in range(len(parts)):
            with eng.Fori(0, share - 1) as j:
                body(part, j, (part, j + 1))
            body(part, share - 1, (part + 1, 0) if part + 1 < len(parts) else None)

    with Sems(nc, name) as S, ExitStack() as ctx:
        def sb(nm, shape, dt=F32):
            return ctx.enter_context(nc.sbuf_tensor(f"{name}_{nm}", shape, dt))

        h_tok, x_tok, x_hat = (sb(n, [MT, 3, D]) for n in ("h_tok", "x_tok", "x_hat"))
        residual, y = sb("residual", [MT, 3, D]), sb("y", [MT, 3, D])
        res_part = sb("res_part", [MT, 3, D])
        xs = SplitX(sb, "x", MW)
        x_aff_a, x_aff_b = sb("x_aff_a", [P, MW]), sb("x_aff_b", [DB, MW])
        hid = [sb(f"hid{p}", [P, chunks, MW]) for p in range(2)]
        pre_stats, stats = sb("pre_stats", [MT, 3, 6]), sb("stats", [MT, 3, 6])
        pre_mv, mean_var = sb("pre_mv", [MT, 3, 2]), sb("mean_var", [MT, 3, 2])
        pre_var, pre_rstd, var_eps, rstd = (sb(n, [MT, 3]) for n in ("pre_var", "pre_rstd", "var_eps", "rstd"))

        def bank(b):
            return psum[:, b * BANK:(b + 1) * BANK]

        block = ctx.enter_context(nc.Block())

        @block.sync
        def _(sp):
            def load(i):
                sp.wait_ge(S["residual_ready"], i)
                sp.wait_ge(S["x_hat_ready"], i)
                sp.dma_start(x_tok[:, :, :], x_src(i)).then_inc(S["x_loaded"], 16)
                sp.dma_start(h_tok[:, :, :], h_src(i)).then_inc(S["h_loaded"], 16)

            def store(i):
                sp.wait_ge(S["y_ready"], 3 * i + 3)
                sp.dma_start(dst(i), y[:, :, :]).then_inc(S["y_stored"], 16)

            sp.dma_start(x_tok[:, :, :], x_src(0)).then_inc(S["x_loaded"], 16)
            sp.dma_start(h_tok[:, :, :], h_src(0)).then_inc(S["h_loaded"], 16)
            with sp.Fori(0, n_iter - 1) as i:
                load(i + 1)
                store(i)
            store(n_iter - 1)
            sp.wait_ge(S["y_stored"], 16 * n_iter)

        @block.gpsimd
        def _(pool):
            def pre_pow(i):
                pool.wait_ge(S["pre_var_ready"], i + 1)
                nc.gpsimd.tensor_tensor(pre_rstd[:, :], pre_var[:, :], neg_half[:, :], ALU.pow
                                        ).then_inc(S["pre_rstd_ready"], 1)

            def make_residual(i, part):
                out_bias = parts[part][1]
                pool.wait_ge(S["x_loaded"], 16 * i + 16)
                pool.wait_ge(S["h_loaded"], 16 * i + 16)
                nc.gpsimd.tensor_tensor(res_part[:, :, :], x_tok[:, :, :], h_tok[:, :, :], ALU.add
                                        ).then_inc(S["res_part_ready"], 1)
                pool.wait_ge(S["res_part_ready"], i + 1)
                pool.wait_ge(S["mlp_added"], 3 * i)
                nc.gpsimd.tensor_tensor(residual[:, :, :], res_part[:, :, :],
                                        out_bias.rearrange("p (a n) -> p a n", a=1)
                                        .to_broadcast([MT, 3, D]), ALU.add
                                        ).then_inc(S["residual_ready"], 1)

            def out_pow(i, t):
                pool.wait_ge(S["var_ready"], 3 * i + t + 1)
                nc.gpsimd.tensor_tensor(rstd[:, t:t + 1], var_eps[:, t:t + 1], neg_half[:, 0:1], ALU.pow
                                        ).then_inc(S["rstd_ready"], 1)

            def body(part, j, following):
                i = part * share + j
                make_residual(i, part)
                if following:
                    pre_pow(i + 1)
                for t in range(3):
                    out_pow(i, t)

            pre_pow(0)
            over_iterations(pool, body)

        @block.tensor
        def _(pe):
            def transpose_x(i):
                pe.wait_ge(S["x_hat_ready"], i + 1)
                for t in range(3):
                    nc.tensor.transpose(bank(6)[:, t * MT:(t + 1) * MT], x_hat[:, t, 0:P], ident[:, :])
                    last = nc.tensor.transpose(bank(7)[0:DB, t * MT:(t + 1) * MT], x_hat[:, t, P:D],
                                               ident[:, :])
                last.then_inc(S["x_transposed"], 1)

            def up(part, j, br):
                i, first = part * share + j, before(part, j)
                kept = parts[part][0][br][0]
                for c in range(chunks):
                    n = br * chunks + c
                    if n == 0:
                        pe.wait_ge(S["x_split"], i + 1)
                        pe.wait_ge(S["gelu_done"], first)
                    elif n >= 3:
                        pe.wait_ge(S["gelu_done"], first + n - 2)
                    out, cols = bank(n % 3)[:, 0:MW], slice(c * P, (c + 1) * P)
                    if kept == D:
                        ins = weight_by_x(nc, out, w_up, cols, xs, slice(0, MW))
                    else:
                        ins = weight_by_x_head(nc, out, w_up, cols, xs, slice(0, MW), kept)
                    ins.then_inc(S["up_done"], 1)

            def down(part, j, br):
                i, first = part * share + j, before(part, j)
                branches = parts[part][0]
                w = branches[br][1]
                if br == 0:
                    pe.wait_ge(S["mlp_added"], 3 * i)
                final = br == len(branches) - 1
                for t in range(3):
                    for c in range(chunks):
                        if t == 0:
                            pe.wait_ge(S["gelu_done"], first + br * chunks + c + 1)
                        last = nc.tensor.matmul(bank(3 + t)[:, 0:w.shape[2]],
                                                hid[br % 2][:, c, t * MT:(t + 1) * MT], w[:, c, :],
                                                start=(br == 0 and c == 0), stop=(final and c == chunks - 1))
                    if final:
                        last.then_inc(S["down_done"], 1)

            def body(part, j, following):
                branches = len(parts[part][0])
                up(part, j, 0)
                for br in range(1, branches):
                    up(part, j, br)
                    down(part, j, br - 1)
                if following:
                    transpose_x(part * share + j + 1)
                down(part, j, branches - 1)

            transpose_x(0)
            over_iterations(pe, body)

        @block.scalar
        def _(act):
            def round_x(part, j):
                act.wait_ge(S["x_transposed"], part * share + j + 1)
                ga, gb, ba, bb = parts[part][2]
                nc.scalar.activation(xs.a_hi[:, :], bank(6)[:, 0:MW], ACT.Identity, bias=ba, scale=ga
                                     ).then_inc(S["x_rounded"], 1)
                nc.scalar.activation(xs.b[0:DB, :], bank(7)[0:DB, 0:MW], ACT.Identity, bias=bb, scale=gb
                                     ).then_inc(S["x_rounded"], 1)

            def gelu(part, j):
                for n in range(per_iter[part]):
                    act.wait_ge(S["up_done"], before(part, j) + n + 1)
                    c = n % chunks
                    nc.scalar.activation(hid[(n // chunks) % 2][:, c, :], bank(n % 3)[:, 0:MW], ACT.Gelu,
                                         bias=b_up[:, c:c + 1]).then_inc(S["gelu_done"], 1)

            def body(part, j, following):
                gelu(part, j)
                if following:
                    round_x(*following)

            round_x(0, 0)
            over_iterations(act, body)

        @block.vector
        def _(dve):
            def pre_norm(i):
                dve.wait_ge(S["x_loaded"], 16 * i + 16)
                for t in range(3):
                    nc.vector.bn_stats(pre_stats[:, t, :], x_tok[:, t, :]).then_inc(S["pre_stats_ready"], 1)
                for t in range(3):
                    wait_apart(dve, S["pre_stats_ready"], 3 * i + t + 1)
                    nc.vector.bn_aggr(pre_mv[:, t, :], pre_stats[:, t, :]).then_inc(S["pre_mv_ready"], 1)
                dve.wait_ge(S["pre_mv_ready"], 3 * i + 3)
                nc.vector.tensor_scalar(pre_var[:, :], pre_mv[:, :, 1], EPS, None, ALU.add
                                        ).then_inc(S["pre_var_ready"], 1)
                dve.wait_ge(S["pre_rstd_ready"], i + 1)
                dve.wait_ge(S["x_transposed"], i)
                for t in range(3):
                    last = nc.vector.tensor_scalar(x_hat[:, t, :], x_tok[:, t, :], pre_mv[:, t, 0:1],
                                                   pre_rstd[:, t:t + 1], ALU.subtract, ALU.mult)
                last.then_inc(S["x_hat_ready"], 1)

            def split_x(part, j):
                i = part * share + j
                ga, gb, ba, bb = parts[part][2]
                dve.wait_ge(S["x_rounded"], 2 * i + 2)
                nc.vector.tensor_scalar(x_aff_a[:, :], bank(6)[:, 0:MW], ga, ba, ALU.mult, ALU.add
                                        ).then_inc(S["x_affine"], 1)
                nc.vector.tensor_scalar(x_aff_b[:, :], bank(7)[0:DB, 0:MW], gb, bb, ALU.mult, ALU.add
                                        ).then_inc(S["x_affine"], 1)
                dve.wait_ge(S["x_affine"], 2 * i + 2)
                nc.vector.tensor_tensor(xs.a_lo[:, :], x_aff_a[:, :], xs.a_hi[:, :].bitcast(F32),
                                        ALU.subtract)
                nc.vector.tensor_tensor(xs.b[DB:P, :], x_aff_b[:, :], xs.b[0:DB, :].bitcast(F32),
                                        ALU.subtract).then_inc(S["x_split"], 1)

            def add_residual(i, t):
                n = 3 * i + t + 1
                dve.wait_ge(S["down_done"], n)
                if t == 0:
                    dve.wait_ge(S["residual_ready"], i + 1)
                    dve.wait_ge(S["y_stored"], 16 * i)
                nc.vector.tensor_tensor(y[:, t, :], bank(3 + t)[:, 0:D], residual[:, t, :], ALU.add
                                        ).then_inc(S["mlp_added"], 1)
                dve.wait_ge(S["mlp_added"], n)
                nc.vector.bn_stats(stats[:, t, :], y[:, t, :]).then_inc(S["stats_ready"], 1)
                wait_apart(dve, S["stats_ready"], n)
                nc.vector.bn_aggr(mean_var[:, t, :], stats[:, t, :]).then_inc(S["mean_ready"], 1)
                dve.wait_ge(S["mean_ready"], n)
                nc.vector.tensor_scalar(var_eps[:, t:t + 1], mean_var[:, t, 1:2], EPS, None, ALU.add
                                        ).then_inc(S["var_ready"], 1)

            def post_norm(i, t):
                dve.wait_ge(S["rstd_ready"], 3 * i + t + 1)
                nc.vector.tensor_scalar(y[:, t, :], y[:, t, :], mean_var[:, t, 0:1], rstd[:, t:t + 1],
                                        ALU.subtract, ALU.mult).then_inc(S["y_ready"], 1)

            def body(part, j, following):
                i = part * share + j
                if following:
                    pre_norm(i + 1)
                    split_x(*following)
                add_residual(i, 0)
                add_residual(i, 1)
                post_norm(i, 0)
                add_residual(i, 2)
                post_norm(i, 1)
                post_norm(i, 2)

            pre_norm(0)
            split_x(0, 0)
            over_iterations(dve, body)



def moe_stage(nc, psum, ident, neg_half, name, src, dst, n_iter, w_gu, w_router, sg_bias, w_dn_shared,
              w_dn, w_dn_mid, iota8):
    sh = HID // P
    pair = 2 * D // P
    groups = [(0, sh)] + [(sh + pair * n, pair) for n in range(EXPERTS // 2)]
    total = sh + EH // P
    outs = 3 * (1 + EXPERTS)

    def gate_col(c):
        return c * P if c < sh else 2 * HID + (c - sh) * P

    def up_col(c):
        return HID + c * P if c < sh else 2 * HID + EH + (c - sh) * P

    with Sems(nc, name) as S, ExitStack() as ctx:
        def sb(nm, shape, dt=F32):
            return ctx.enter_context(nc.sbuf_tensor(f"{name}_{nm}", shape, dt))

        h_tok, acc, y = (sb(n, [MT, 3, D]) for n in ("h_tok", "acc", "y"))
        xs = SplitX(sb, "x", MW)
        silu = [sb(f"silu{p}", [P, MW]) for p in range(2)]
        hid_shared = sb("hid_shared", [P, sh, MW])
        hid_pair = [sb(f"hid_pair{p}", [P, pair, MW]) for p in range(2)]
        logits = sb("logits", [MT, 3, 10])
        top8 = sb("top8", [MT, 3, 8])
        index = sb("index", [MT, 3, 8], U32)
        index_f = sb("index_f", [MT, 3, 2])
        pre_tanh, tanh = sb("pre_tanh", [MT, 2, 3]), sb("tanh", [MT, 2, 3])
        plus, minus = sb("plus", [MT, 2, 3]), sb("minus", [MT, 2, 3])
        gate1, gate2 = sb("gate1", [MT, 3]), sb("gate2", [MT, 3])
        coef1, coef = sb("coef1", [MT, 3, 8]), sb("coef", [MT, 3, 8])
        alpha = sb("alpha", [MT, 3])
        stats, mean_var = sb("stats", [MT, 3, 6]), sb("mean_var", [MT, 3, 2])
        var_eps, rstd = sb("var_eps", [MT, 3]), sb("rstd", [MT, 3])

        def hid(gr):
            return hid_shared if gr == 0 else hid_pair[(gr - 1) % 2]

        def bank(b):
            return psum[:, b * BANK:(b + 1) * BANK]

        def down_ps(n):
            return bank(4 + n % 2)[:, 0:D]

        block = ctx.enter_context(nc.Block())

        @block.sync
        def _(sp):
            def load_next(i):
                sp.wait_ge(S["x_transposed"], i + 1)
                sp.wait_ge(S["combined"], outs * i + 3)
                sp.dma_start(h_tok[:, :, :], src(i + 1)).then_inc(S["h_loaded"], 16)

            def store(i):
                sp.wait_ge(S["y_ready"], 3 * i + 3)
                sp.dma_start(dst(i), y[:, :, :]).then_inc(S["y_stored"], 16)

            sp.dma_start(h_tok[:, :, :], src(0)).then_inc(S["h_loaded"], 16)
            with sp.Fori(0, n_iter - 1) as i:
                load_next(i)
                store(i)
            store(n_iter - 1)
            sp.wait_ge(S["y_stored"], 16 * n_iter)

        @block.gpsimd
        def _(pool):
            with pool.Fori(0, n_iter) as i:
                pool.wait_ge(S["var_ready"], i + 1)
                nc.gpsimd.tensor_tensor(rstd[:, :], var_eps[:, :], neg_half[:, :], ALU.pow
                                        ).then_inc(S["rstd_ready"], 1)

        @block.tensor
        def _(pe):
            def transpose_x(i):
                pe.wait_ge(S["h_loaded"], 16 * i + 16)
                pe.wait_ge(S["logits_copied"], i)
                for t in range(3):
                    nc.tensor.transpose(bank(6)[:, t * MT:(t + 1) * MT], h_tok[:, t, 0:P], ident[:, :])
                    last = nc.tensor.transpose(bank(7)[0:DB, t * MT:(t + 1) * MT], h_tok[:, t, P:D],
                                               ident[:, :])
                last.then_inc(S["x_transposed"], 1)

            def route(i):
                pe.wait_ge(S["x_split"], i + 1)
                for t in range(3):
                    last = x_by_weight(nc, bank(6)[:, t * 10:t * 10 + 10], xs, slice(t * MT, (t + 1) * MT),
                                       w_router, slice(0, 10))
                last.then_inc(S["logits_done"], 1)

            def gate_up(i, gr):
                first, count = groups[gr]
                for c in range(first, first + count):
                    if c == 0:
                        pe.wait_ge(S["x_split"], i + 1)
                    if c >= 2:
                        pe.wait_ge(S["hid_ready"], total * i + c - 1)
                    else:
                        pe.wait_ge(S["hid_ready"], total * i)
                    b = 2 * (c % 2)
                    weight_by_x(nc, bank(b)[:, 0:MW], w_gu, slice(gate_col(c), gate_col(c) + P), xs,
                                slice(0, MW)).then_inc(S["gate_done"], 1)
                    weight_by_x(nc, bank(b + 1)[:, 0:MW], w_gu, slice(up_col(c), up_col(c) + P), xs,
                                slice(0, MW)).then_inc(S["up_done"], 1)

            def down(i, gr):
                first, count = groups[gr]
                pe.wait_ge(S["hid_ready"], total * i + first + count)
                if gr == 0:
                    sums = [[(c, w_dn_shared[:, c, :]) for c in range(sh)]]
                else:
                    k = gr - 1
                    sums = [[(0, w_dn[:, 3 * k, :]), (1, w_dn_mid[:, 2 * k, :])],
                            [(1, w_dn_mid[:, 2 * k + 1, :]), (2, w_dn[:, 3 * k + 2, :])]]
                for e, terms in enumerate(sums):
                    for t in range(3):
                        n = 3 * (0 if gr == 0 else 2 * gr - 1 + e) + t
                        pe.wait_ge(S["combined"], outs * i + max(0, n - 1))
                        for m, (c, w) in enumerate(terms):
                            last = nc.tensor.matmul(down_ps(n),
                                                    hid(gr)[:, c, t * MT:(t + 1) * MT], w,
                                                    start=(m == 0), stop=(m == len(terms) - 1))
                        last.then_inc(S["down_done"], 1)

            def body(i, last):
                gate_up(i, 0)
                gate_up(i, 1)
                down(i, 0)
                gate_up(i, 2)
                down(i, 1)
                gate_up(i, 3)
                down(i, 2)
                gate_up(i, 4)
                if not last:
                    transpose_x(i + 1)
                down(i, 3)
                if not last:
                    route(i + 1)
                down(i, 4)

            transpose_x(0)
            route(0)
            with pe.Fori(0, n_iter - 1) as i:
                body(i, False)
            body(n_iter - 1, True)

        @block.scalar
        def _(act):
            def round_x(i):
                act.wait_ge(S["x_transposed"], i + 1)
                nc.scalar.activation(xs.a_hi[:, :], bank(6)[:, 0:MW], ACT.Copy).then_inc(S["x_rounded"], 1)
                nc.scalar.activation(xs.b[0:DB, :], bank(7)[0:DB, 0:MW], ACT.Copy
                                     ).then_inc(S["x_rounded"], 1)

            def gates(i):
                act.wait_ge(S["pre_tanh_ready"], 2 * i + 2)
                nc.scalar.activation(tanh[:, :, :], pre_tanh[:, :, :], ACT.Tanh, scale=0.5
                                     ).then_inc(S["tanh_ready"], 1)

            def silus(i):
                for c in range(total):
                    act.wait_ge(S["gate_done"], total * i + c + 1)
                    if c >= 2:
                        act.wait_ge(S["hid_ready"], total * i + c - 1)
                    nc.scalar.activation(silu[c % 2][:, :], bank(2 * (c % 2))[:, 0:MW], ACT.Silu
                                         ).then_inc(S["silu_done"], 1)
                    if c == 2:
                        gates(i)

            round_x(0)
            with act.Fori(0, n_iter - 1) as i:
                silus(i)
                round_x(i + 1)
            silus(n_iter - 1)

        @block.vector
        def _(dve):
            def split_x(i):
                dve.wait_ge(S["x_rounded"], 2 * i + 2)
                nc.vector.tensor_tensor(xs.a_lo[:, :], bank(6)[:, 0:MW], xs.a_hi[:, :].bitcast(F32),
                                        ALU.subtract)
                nc.vector.tensor_tensor(xs.b[DB:P, :], bank(7)[0:DB, 0:MW], xs.b[0:DB, :].bitcast(F32),
                                        ALU.subtract).then_inc(S["x_split"], 1)

            def top_two(i):
                dve.wait_ge(S["logits_done"], i + 1)
                nc.vector.tensor_copy(logits[:, :, :], bank(6)[:, 0:30].rearrange("p (t n) -> p t n", t=3)
                                      ).then_inc(S["logits_copied"], 1)
                dve.wait_ge(S["logits_copied"], i + 1)
                nc.vector.tensor_scalar(pre_tanh[:, 1, :], logits[:, :, 8], sg_bias, None, ALU.add
                                        ).then_inc(S["pre_tanh_ready"], 1)
                for t in range(3):
                    nc.vector.max(top8[:, t, :], logits[:, t, 0:8]).then_inc(S["top_ready"], 1)
                dve.wait_ge(S["top_ready"], 3 * i + 3)
                nc.vector.tensor_tensor(pre_tanh[:, 0, :], top8[:, :, 0], top8[:, :, 1], ALU.subtract
                                        ).then_inc(S["pre_tanh_ready"], 1)
                for t in range(3):
                    nc.vector.max_index(index[:, t, :], top8[:, t, :], logits[:, t, 0:8]
                                        ).then_inc(S["index_ready"], 1)
                dve.wait_ge(S["index_ready"], 3 * i + 3)
                nc.vector.tensor_copy(index_f[:, :, :], index[:, :, 0:2]).then_inc(S["index_f_ready"], 1)

            def sigmoids(i):
                dve.wait_ge(S["tanh_ready"], i + 1)
                nc.vector.tensor_scalar(plus[:, :, :], tanh[:, :, :], 0.5, 0.5, ALU.mult, ALU.add
                                        ).then_inc(S["sigmoids_ready"], 1)
                nc.vector.tensor_scalar(minus[:, :, :], tanh[:, :, :], -0.5, 0.5, ALU.mult, ALU.add
                                        ).then_inc(S["sigmoids_ready"], 1)
                dve.wait_ge(S["sigmoids_ready"], 2 * i + 2)
                nc.vector.tensor_copy(alpha[:, :], plus[:, 1, :]).then_inc(S["gates_ready"], 1)
                nc.vector.tensor_tensor(gate1[:, :], plus[:, 0, :], minus[:, 1, :], ALU.mult
                                        ).then_inc(S["gates_ready"], 1)
                nc.vector.tensor_tensor(gate2[:, :], minus[:, 0, :], minus[:, 1, :], ALU.mult
                                        ).then_inc(S["gates_ready"], 1)

            def coefficients(i):
                dve.wait_ge(S["gates_ready"], 3 * i + 3)
                dve.wait_ge(S["index_f_ready"], i + 1)
                for t in range(3):
                    nc.vector.tensor_scalar(coef1[:, t, :], iota8, index_f[:, t, 0:1], gate1[:, t:t + 1],
                                            ALU.is_equal, ALU.mult).then_inc(S["coef_parts_ready"], 1)
                    nc.vector.tensor_scalar(coef[:, t, :], iota8, index_f[:, t, 1:2], gate2[:, t:t + 1],
                                            ALU.is_equal, ALU.mult).then_inc(S["coef_parts_ready"], 1)
                dve.wait_ge(S["coef_parts_ready"], 6 * i + 6)
                nc.vector.tensor_tensor(coef[:, :, :], coef[:, :, :], coef1[:, :, :], ALU.add
                                        ).then_inc(S["coef_ready"], 1)
                dve.wait_ge(S["coef_ready"], i + 1)

            def multiply_chunk(i, gr, c):
                dve.wait_ge(S["silu_done"], total * i + c + 1)
                dve.wait_ge(S["up_done"], total * i + c + 1)
                nc.vector.tensor_tensor(hid(gr)[:, c - groups[gr][0], :], bank(2 * (c % 2) + 1)[:, 0:MW],
                                        silu[c % 2][:, :], ALU.mult).then_inc(S["hid_ready"], 1)

            def multiply(i, gr):
                first, count = groups[gr]
                for c in range(first, first + count):
                    multiply_chunk(i, gr, c)

            def combine(i, gr):
                for e in ([0] if gr == 0 else [2 * gr - 1, 2 * gr]):
                    for t in range(3):
                        n = 3 * e + t
                        dve.wait_ge(S["down_done"], outs * i + n + 1)
                        if e > 0:
                            dve.wait_ge(S["combined"], outs * i + n - 2)
                        scalar = alpha[:, t:t + 1] if e == 0 else coef[:, t, e - 1:e]
                        ins = nc.vector.scalar_tensor_tensor(
                            out=acc[:, t, :], in0=down_ps(n), scalar=scalar,
                            in1=(h_tok if e == 0 else acc)[:, t, :], op0=ALU.mult, op1=ALU.add)
                        ins.then_inc(S["combined"], 1)

            def output_stats(i):
                dve.wait_ge(S["combined"], outs * i + outs)
                for t in range(3):
                    nc.vector.bn_stats(stats[:, t, :], acc[:, t, :]).then_inc(S["stats_ready"], 1)
                for t in range(3):
                    wait_apart(dve, S["stats_ready"], 3 * i + t + 1)
                    nc.vector.bn_aggr(mean_var[:, t, :], stats[:, t, :]).then_inc(S["mean_ready"], 1)
                dve.wait_ge(S["mean_ready"], 3 * i + 3)
                nc.vector.tensor_scalar(var_eps[:, :], mean_var[:, :, 1], EPS, None, ALU.add
                                        ).then_inc(S["var_ready"], 1)

            def normalise(i):
                dve.wait_ge(S["y_stored"], 16 * i)
                dve.wait_ge(S["rstd_ready"], i + 1)
                for t in range(3):
                    nc.vector.tensor_scalar(y[:, t, :], acc[:, t, :], mean_var[:, t, 0:1], rstd[:, t:t + 1],
                                            ALU.subtract, ALU.mult).then_inc(S["y_ready"], 1)

            def shared_chunks(i, pieces):
                for c in range(sh):
                    multiply_chunk(i, 0, c)
                    if c < len(pieces):
                        pieces[c]()

            def body(i, last):
                multiply(i, 1)
                combine(i, 0)
                multiply(i, 2)
                combine(i, 1)
                multiply(i, 3)
                combine(i, 2)
                multiply(i, 4)
                if not last:
                    split_x(i + 1)
                combine(i, 3)
                combine(i, 4)
                if last:
                    output_stats(i)
                    normalise(i)
                else:
                    shared_chunks(i + 1, [lambda: output_stats(i), lambda: top_two(i + 1),
                                          lambda: normalise(i), lambda: sigmoids(i + 1),
                                          lambda: coefficients(i + 1)])

            split_x(0)
            shared_chunks(0, [lambda: top_two(0), lambda: None, lambda: sigmoids(0),
                              lambda: coefficients(0)])
            with dve.Fori(0, n_iter - 1) as i:
                body(i, False)
            body(n_iter - 1, True)



def padded(cols, width, pad):
    return cols.rearrange("p (h r) -> p h r", r=pad)[:, :, 0:width]


def split_views(w, at, n, width=None, pad=None):
    out = [t[:, at:at + n] for t in (w.a_hi, w.a_lo, w.b_hi, w.b_lo)]
    return [padded(t, width, pad) for t in out] if pad else out


def part_views(src, first, n, width):
    cols = src[:, first:first + n]
    return cols.rearrange("p (h e) -> p h e", e=width) if width else cols


def remainder_weight_jobs(nc, which, eng, S, stage_a, stage_b, jobs):
    for j, (_, n, parts) in enumerate(jobs):
        for stage, view, p in ((stage_a, 0, P), (stage_b, 2, DB)):
            eng.wait_ge(S["weight_hi_done"], 2 * j + (2 if view else 1))
            for first, count, views, width in parts:
                last = which.tensor_tensor(views[view + 1],
                                           part_views(stage[j % 2], first, count, width)[0:p],
                                           views[view][0:p].bitcast(F32), ALU.subtract)
            last.then_inc(S["weight_lo_done"], 1)


def load_one(eng, S, stage_a, stage_b, jobs, j):
    dram, n, _ = jobs[j]
    if j >= 2:
        eng.wait_ge(S["weight_lo_done"], 2 * (j - 1))
    eng.dma_start(stage_a[j % 2][:, 0:n], dram[0:P]).then_inc(S["weight_loaded%d" % (j % 2)], 16)
    for half in range(2):
        eng.dma_start(stage_b[j % 2][half * DB:(half + 1) * DB, 0:n], dram[P:D]
                      ).then_inc(S["weight_loaded%d" % (j % 2)], 16)


def round_one(nc, eng, S, stage_a, stage_b, jobs, j):
    _, n, parts = jobs[j]
    eng.wait_ge(S["weight_loaded%d" % (j % 2)], 48 * (j // 2 + 1))
    if j == 0:
        eng.wait_ge(S["pads_cleared"], PADS)
    for stage, view in ((stage_a, 0), (stage_b, 2)):
        for first, count, views, width in parts:
            last = nc.scalar.activation(views[view], part_views(stage[j % 2], first, count, width),
                                        ACT.Copy)
        last.then_inc(S["weight_hi_done"], 1)


def embed_stage(nc, psum, name, patches_t, w_tok, w_tok_dram, pos_rows, b_rows, dst, jobs,
                prepare):
    n_iter, chunks = TOK // WIDE, PATCH_K // P
    with Sems(nc, name) as S, ExitStack() as ctx:
        def sb(nm, shape, dt=F32):
            return ctx.enter_context(nc.sbuf_tensor(f"{name}_{nm}", shape, dt))

        patches = [sb(f"patches{p}", [P, chunks, WIDE]) for p in range(2)]
        pos = sb("pos", [TILE, TILES, D])
        b_tok = sb("b_tok", [TILE, D])
        pos_b = sb("pos_b", [TILE, TILES, D])
        y = [sb(f"y{p}", [TILE, TILES, D]) for p in range(2)]
        stage_a = [sb(f"stage_a{p}", [P, 768]) for p in range(2)]
        stage_b = [sb(f"stage_b{p}", [P, 768]) for p in range(2)]

        def out_bank(n):
            return psum[0:TILE, n * BANK:n * BANK + D]

        prep = prepare(S, sb)
        block = ctx.enter_context(nc.Block())

        @block.sync
        def _(sp):
            sp.dma_start(w_tok[:, :, :], w_tok_dram).then_inc(S["tok_weights_loaded"], 16)
            sp.dma_start(pos[:, :, :], pos_rows).then_inc(S["pos_loaded"], 16)
            sp.dma_start(b_tok[:, :], b_rows).then_inc(S["pos_loaded"], 16)
            sp.dma_start(patches[0][:, :, :], patches_t(0)).then_inc(S["patches_loaded0"], 16)

            def step(j, p, last):
                i = 2 * j + p
                if not last:
                    sp.wait_ge(S["embedded"], TILES * i)
                    sp.dma_start(patches[1 - p][:, :, :], patches_t(i + 1)
                                 ).then_inc(S[f"patches_loaded{1 - p}"], 16)
                sp.wait_ge(S[f"y_ready{p}"], TILES * (j + 1))
                sp.dma_start(dst(i), y[p][:, :, :]).then_inc(S[f"y_stored{p}"], 16)

            with sp.Fori(0, n_iter // 2 - 1) as j:
                step(j, 0, False)
                step(j, 1, False)
            step(n_iter // 2 - 1, 0, False)
            step(n_iter // 2 - 1, 1, True)
            sp.wait_ge(S["y_stored0"], 16 * (n_iter // 2))
            sp.wait_ge(S["y_stored1"], 16 * (n_iter // 2))
            prep["sync"](sp)

        @block.tensor
        def _(pe):
            pe.wait_ge(S["tok_weights_loaded"], 16)

            def step(j, p):
                i = 2 * j + p
                pe.wait_ge(S[f"patches_loaded{p}"], 16 * j + 16)
                for t in range(TILES):
                    pe.wait_ge(S[f"y_ready{p}"], TILES * j)
                    for c in range(chunks):
                        last = nc.tensor.matmul(out_bank(TILES * p + t), patches[p][:, c, t * TILE:(t + 1) * TILE],
                                                w_tok[:, c, :], start=(c == 0), stop=(c == chunks - 1))
                    last.then_inc(S["embedded"], 1)

            with pe.Fori(0, n_iter // 2) as j:
                step(j, 0)
                step(j, 1)
            prep["tensor"](pe)

        @block.vector
        def _(dve):
            dve.wait_ge(S["pos_loaded"], 32)
            nc.vector.tensor_tensor(pos_b[:, :, :], pos[:, :, :],
                                    b_tok[:, :].rearrange("p (a n) -> p a n", a=1)
                                    .to_broadcast([TILE, TILES, D]), ALU.add
                                    ).then_inc(S["pos_bias_ready"], 1)
            dve.wait_ge(S["pos_bias_ready"], 1)
            prep["vector_start"](dve)

            def step(j, p):
                i = 2 * j + p
                dve.wait_ge(S[f"y_stored{p}"], 16 * j)
                for t in range(TILES):
                    dve.wait_ge(S["embedded"], TILES * i + t + 1)
                    nc.vector.tensor_tensor(y[p][:, t, :], out_bank(TILES * p + t), pos_b[:, t, :],
                                            ALU.add).then_inc(S[f"y_ready{p}"], 1)

            with dve.Fori(0, n_iter // 4) as j:
                step(j, 0)
                step(j, 1)
            prep["vector_middle"](dve)
            with dve.Fori(n_iter // 4, n_iter // 2) as j:
                step(j, 0)
                step(j, 1)
            prep["vector"](dve)

        @block.scalar
        def _(act):
            for j in range(2):
                load_one(act, S, stage_a, stage_b, jobs, j)
            prep["scalar_loads"](act)
            for j in range(len(jobs)):
                round_one(nc, act, S, stage_a, stage_b, jobs, j)
                if j + 2 < len(jobs):
                    load_one(act, S, stage_a, stage_b, jobs, j + 2)
            prep["scalar"](act)

        @block.gpsimd
        def _(pool):
            prep["gpsimd"](pool)
            remainder_weight_jobs(nc, nc.gpsimd, pool, S, stage_a, stage_b, jobs)


class MoeWeights:

    STEPS = TOK // WIDE

    def __init__(self, nc, ctx, sb, w_gu, w_gu_dram, w_dn_shared, ws_down, w_dn, w_down, w_dn_mid):
        self.nc, self.w_gu, self.w_gu_dram = nc, w_gu, w_gu_dram
        self.n = w_gu.n // self.STEPS
        self.raw_a, self.raw_b = sb("raw_a", [P, self.n]), sb("raw_b", [P, self.n])
        self.down = (w_dn_shared, ws_down, w_dn, w_down, w_dn_mid)
        self.raw_loaded = ctx.enter_context(nc.semaphore("moe_raw_loaded"))
        self.down_loaded = ctx.enter_context(nc.semaphore("moe_down_loaded"))
        self.cleared = ctx.enter_context(nc.semaphore("moe_mid_cleared"))
        self.rounded = ctx.enter_context(nc.semaphore("moe_rounded"))
        self.split = ctx.enter_context(nc.semaphore("moe_split"))

    def load_start(self, sp):
        w_dn_shared, ws_down, w_dn, w_down, w_dn_mid = self.down
        chunks = w_down.rearrange("(c p) n -> c p n", p=P)
        sp.dma_start(w_dn_shared[:, :, :], ws_down.rearrange("(c p) n -> p c n", p=P)
                     ).then_inc(self.down_loaded, 16)
        sp.dma_start(w_dn[:, :, :], chunks.rearrange("c p n -> p c n")).then_inc(self.down_loaded, 16)
        sp.wait_ge(self.cleared, 1)
        for k in range(EXPERTS // 2):
            for half in range(2):
                rows_ = slice(half * DB, (half + 1) * DB)
                sp.dma_start(w_dn_mid[rows_, 2 * k + half, :], chunks[3 * k + 1][rows_]
                             ).then_inc(self.down_loaded, 16)
        sp.wait_ge(self.down_loaded, 16 * (2 + EXPERTS))

    def load_step(self, sp, i):
        sp.wait_ge(self.split, 2 * i)
        cols = bass.ds(i * self.n, self.n)
        sp.dma_start(self.raw_a[:, :], self.w_gu_dram[0:P, cols]).then_inc(self.raw_loaded, 16)
        for half in range(2):
            sp.dma_start(self.raw_b[half * DB:(half + 1) * DB, :], self.w_gu_dram[P:D, cols]
                         ).then_inc(self.raw_loaded, 16)

    def split_start(self, pool):
        self.nc.gpsimd.memset(self.down[4][:, :, :], 0.0).then_inc(self.cleared, 1)

    def round_step(self, act, i):
        nc, w, cols = self.nc, self.w_gu, bass.ds(i * self.n, self.n)
        act.wait_ge(self.raw_loaded, 48 * i + 48)
        nc.scalar.activation(w.a_hi[:, cols], self.raw_a[:, :], ACT.Copy).then_inc(self.rounded, 1)
        nc.scalar.activation(w.b_hi[:, cols], self.raw_b[:, :], ACT.Copy).then_inc(self.rounded, 1)

    def split_step(self, pool, i):
        nc, w, cols = self.nc, self.w_gu, bass.ds(i * self.n, self.n)
        pool.wait_ge(self.rounded, 2 * i + 2)
        nc.gpsimd.tensor_tensor(w.a_lo[:, cols], self.raw_a[:, :], w.a_hi[:, cols].bitcast(F32),
                                ALU.subtract).then_inc(self.split, 1)
        nc.gpsimd.tensor_tensor(w.b_lo[:, cols], self.raw_b[0:DB, :], w.b_hi[0:DB, cols].bitcast(F32),
                                ALU.subtract).then_inc(self.split, 1)


PADS = 16


def build(nc, x, tok_w, tok_b, pos, wq1, wk1, wv1, w_qkv2, w_fc1, w_fc2, w_qkv3, columns_dram,
          vectors_dram, w_out_dram, w_gu_dram, w_router_dram, w_down, ws_down, out):
    top = ExitStack()
    h = [nc.dram_tensor(f"h{i}", [TOK, D], F32, kind="Internal").ap() for i in range(4)]
    x1 = nc.dram_tensor("x1", [TOK, D], F32, kind="Internal").ap()
    def tiles(a, p):
        view = a.rearrange("(i t p) d -> i p t d", t=3, p=p)
        return lambda i: view[i]

    with top:
        def sb(nm, shape, dt=F32):
            return top.enter_context(nc.sbuf_tensor(nm, shape, dt))

        psum = top.enter_context(nc.psum_tensor("psum", [P, 8 * BANK], F32))
        ident = sb("ident", [P, P])
        neg_half = sb("neg_half", [P, TILES])
        columns, vectors = sb("columns", [P, 49]), sb("vectors", [P, 4 * D + 4])
        norm_a, norm_b = columns[:, 0:8], columns[0:DB, 8:16]
        q_bias1, k_bias1, bv_cols1, b_up2 = (columns[:, 16 + 6 * n:22 + 6 * n] for n in range(4))
        q_bias3, k_bias3, bv_cols3 = (columns[:, 40 + 3 * n:43 + 3 * n] for n in range(3))
        out_bias1, out_bias2, out_bias3 = (vectors[0:TILE, n * D:(n + 1) * D] for n in range(3))
        b_dn2 = vectors[:, 3 * D:4 * D]
        g, sg_bias = vectors[:, 4 * D:4 * D + 3], vectors[:, 4 * D + 3:4 * D + 4]
        w_o3 = sb("w_o3", [P, 3, D])
        bias3 = sb("bias3", [UNIT, HEADS, UNIT])
        w_router = Split(sb, "w_router", 10)
        iota8 = sb("iota8", [P, EXPERTS])
        w_q3, w_k3, w_v3 = Split(sb, "w_q3", 384), Split(sb, "w_k3", 384), Split(sb, "w_v3", D)

        with ExitStack() as early:
            def esb(nm, shape, dt=F32):
                return early.enter_context(nc.sbuf_tensor(nm, shape, dt))

            w_tok = esb("w_tok", [P, 6, D])
            w_o1, w_o2, w_o2s = esb("w_o1", [P, 6, D]), esb("w_o2", [P, 3, D]), esb("w_o2s", [P, 3, D])
            bias1, bias2 = (esb(f"bias{n}", [UNIT, HEADS, UNIT]) for n in (1, 2))
            out_bias2s = esb("out_bias2s", [TILE, D])
            w_q1, w_k1, w_v1 = (Split(esb, n, HID) for n in ("w_q1", "w_k1", "w_v1"))
            w_q2, w_k2, w_v2 = Split(esb, "w_q2", 384), Split(esb, "w_k2", 384), Split(esb, "w_v2", D)
            w_up2 = Split(esb, "w_up2", HID)
            w_dn2 = esb("w_dn2", [P, 6, D])
            w_dn2s = [esb(f"w_dn2s{n}", [P, 6, D // (n + 1)]) for n in range(3)]
            b_dn2s = esb("b_dn2s", [P, D])

            def plain(w, n):
                return [(0, n, split_views(w, 0, n), None)]

            def qkv_parts(wq, wk, wv):
                return [(0, D, split_views(wq, 0, 384, 16, 32), 16),
                        (D, D, split_views(wk, 0, 384, 16, 32), 16),
                        (2 * D, D, split_views(wv, 0, D), None)]

            jobs = [(wq1, HID, plain(w_q1, HID)), (wk1, HID, plain(w_k1, HID)),
                    (wv1, HID, plain(w_v1, HID)), (w_qkv2, 3 * D, qkv_parts(w_q2, w_k2, w_v2)),
                    (w_fc1, HID, plain(w_up2, HID)), (w_qkv3, 3 * D, qkv_parts(w_q3, w_k3, w_v3)),
                    (w_router_dram, 10, plain(w_router, 10))]

            def prepare(S, ssb):
                distance = ssb("distance", [UNIT, UNIT])
                distance_neg = ssb("distance_neg", [UNIT, UNIT])
                loads = [(columns[:, :], columns_dram), (vectors[:, 0:4 * D + 4], rows(vectors_dram, P))]
                at = 0
                for t in (w_o1, w_o2, w_o3):
                    n = t.shape[1]
                    loads.append((t[:, :, :], w_out_dram.rearrange("c p n -> p c n")[:, at:at + n, :]))
                    at += n
                loads.append((w_dn2[:, :, :], w_fc2.rearrange("(c p) n -> p c n", p=P)))

                def scalar_loads(act):
                    for dst_, src_ in loads:
                        act.dma_start(dst_, src_).then_inc(S["small_loaded"], 16)

                def gpsimd(pool):
                    for w in (w_q2, w_k2, w_q3, w_k3):
                        for t in (w.a_hi, w.a_lo, w.b_hi, w.b_lo):
                            nc.gpsimd.memset(t[:, :].bitcast(F32), 0.0).then_inc(S["pads_cleared"], 1)
                    nc.gpsimd.memset(ident[:, :], 0.0).then_inc(S["const_ready"], 1)
                    nc.gpsimd.memset(neg_half[:, :], -0.5)
                    nc.gpsimd.memset(bias1[:, :, :], 0.0).then_inc(S["const_ready"], 1)
                    nc.gpsimd.memset(bias2[:, :, :], 0.0).then_inc(S["const_ready"], 1)
                    nc.gpsimd.iota(distance[:, :], pattern=[[1, UNIT]], base=0, channel_multiplier=-1,
                                   allow_small_or_imprecise_dtypes=True).then_inc(S["const_ready"], 1)
                    nc.gpsimd.iota(iota8[:, :], pattern=[[1, EXPERTS]], base=0, channel_multiplier=0,
                                   allow_small_or_imprecise_dtypes=True)
                    pool.wait_ge(S["const_ready"], 4)
                    nc.gpsimd.affine_select(out=ident[:, :], in_=ident[:, :], compare_op=ALU.not_equal,
                                            fill=1.0, base=0, pattern=[[-1, P]], channel_multiplier=1
                                            ).then_inc(S["const_ready"], 1)
                    nc.gpsimd.affine_select(out=bias1[:, :, :], in_=bias1[:, :, :], compare_op=ALU.is_ge,
                                            fill=NEG, base=0, pattern=[[0, HEADS], [-1, UNIT]],
                                            channel_multiplier=1).then_inc(S["bias1_causal"], 1)
                    nc.gpsimd.tensor_scalar(distance_neg[:, :], distance[:, :], -1.0, None, ALU.mult
                                            ).then_inc(S["const_ready"], 1)
                    pool.wait_ge(S["const_ready"], 6)
                    pool.wait_ge(S["bias1_causal"], 1)
                    pool.wait_ge(S["slopes_applied"], 1)
                    for t in (bias1, bias2, bias3):
                        first, second = t[:, :, 0:SEQ], t[:, :, SEQ:UNIT]
                        nc.gpsimd.affine_select(out=first, in_=first, compare_op=ALU.is_ge, fill=NEG,
                                                base=SEQ - 1, pattern=[[0, HEADS], [0, SEQ]],
                                                channel_multiplier=-1).then_inc(S["bias_ready"], 1)
                        nc.gpsimd.affine_select(out=second, in_=second, compare_op=ALU.is_ge, fill=NEG,
                                                base=-SEQ, pattern=[[0, HEADS], [0, SEQ]],
                                                channel_multiplier=1).then_inc(S["bias_ready"], 1)

                def tensor(pe):
                    pe.wait_ge(S["small_loaded"], 16 * len(loads))
                    for c in range(6):
                        last = nc.tensor.matmul(psum[0:TILE, 6 * BANK:6 * BANK + D],
                                                bv_cols1[:, c:c + 1].to_broadcast([P, TILE]), w_o1[:, c, :],
                                                start=(c == 0), stop=(c == 5))
                    last.then_inc(S["value_bias_done"], 1)
                    for c in range(3):
                        last = nc.tensor.matmul(psum[0:TILE, 7 * BANK:7 * BANK + D],
                                                bv_cols3[:, c:c + 1].to_broadcast([P, TILE]),
                                                w_o3[:, c, :], start=(c == 0), stop=(c == 2))
                    last.then_inc(S["value_bias_done"], 1)

                def vector_start(dve):
                    dve.wait_ge(S["const_ready"], 6)
                    nc.vector.tensor_tensor(distance[:, :], distance[:, :], distance_neg[:, :], ALU.max
                                            ).then_inc(S["distance_ready"], 1)
                    dve.wait_ge(S["distance_ready"], 1)
                    for hh in range(HEADS):
                        slope = float(np.float32(2.0 ** (-8.0 / HEADS)) ** np.float32(hh + 1))
                        last = nc.vector.tensor_scalar(bias3[:, hh, :], distance[:, :], -slope, None,
                                                       ALU.mult)
                    last.then_inc(S["slopes_applied"], 1)

                def vector_middle(dve):
                    dve.wait_ge(S["small_loaded"], 16 * len(loads))
                    nc.vector.tensor_scalar(q_bias1[:, :], q_bias1[:, :], 1.0 / 8, None, ALU.mult)
                    nc.vector.tensor_scalar(q_bias3[:, :], q_bias3[:, :], 1.0 / 4, None, ALU.mult)
                    S_w = S["small_weights"]
                    n = 0

                    def inc(ins):
                        ins.then_inc(S_w, 1)

                    inc(nc.vector.tensor_scalar(w_o2s[:, :, :], w_o2[:, :, :], g[:, 0:1], None, ALU.mult))
                    inc(nc.vector.tensor_scalar(out_bias2s[:, :], out_bias2[:, :], g[0:TILE, 0:1], None,
                                                ALU.mult))
                    inc(nc.vector.tensor_scalar(b_dn2s[:, :], b_dn2[:, :], g[:, 0:1], None, ALU.mult))
                    n = 3
                    for i, kept in ((1, D // 2), (2, D // 3)):
                        dve.wait_ge(S_w, n)
                        full, tail = divmod(HEADS // (i + 1), 4)
                        pairs = [(w_o2[:, c, :], w_o2s[:, c, :], P) for c in range(full)]
                        if tail:
                            pairs += [(w_o2[:, full, :], w_o2s[:, full, :], 32 * tail)]
                        pairs += [(out_bias2, out_bias2s[:, :], TILE), (b_dn2, b_dn2s[:, :], P)]
                        for whole, part, p in pairs:
                            inc(nc.vector.scalar_tensor_tensor(
                                out=part[0:p, 0:kept], in0=whole[0:p, 0:kept], scalar=g[0:p, i:i + 1],
                                in1=part[0:p, 0:kept], op0=ALU.mult, op1=ALU.add))
                            n += 1
                    for i in range(3):
                        nc.vector.tensor_scalar(w_dn2s[i][:, :, :], w_dn2[:, :, 0:D // (i + 1)],
                                                g[:, i:i + 1], None, ALU.mult)

                def vector(dve):
                    for t, b in ((out_bias1, 6), (out_bias3, 7)):
                        dve.wait_ge(S["value_bias_done"], b - 5)
                        nc.vector.tensor_tensor(t[:, :], psum[0:TILE, b * BANK:b * BANK + D], t[:, :],
                                                ALU.add)

                return {"sync": lambda e: None, "tensor": tensor, "vector": vector, "vector_start": vector_start,
                        "vector_middle": vector_middle, "scalar": lambda e: None,
                        "scalar_loads": scalar_loads, "gpsimd": gpsimd}

            embed_stage(nc, psum, "embed", lambda i: x.rearrange("(c p) (i t) -> i p c t", p=P, t=WIDE)[i],
                        w_tok, tok_w.rearrange("(c p) n -> p c n", p=P), pos, rows(tok_b, TILE),
                        tiles(h[0], TILE), jobs, prepare)
            attention_stage(nc, psum, ident, neg_half, "attn1", tiles(h[0], TILE), tiles(h[1], TILE),
                            TOK // WIDE, 64, 64, w_q1, w_k1, w_v1, bias1, q_bias1, k_bias1, 1 / 8,
                            [(w_o1, out_bias1, None)], True)

            def norm_cols(n):
                return (norm_a[:, n:n + 1], norm_b[:, n:n + 1], norm_a[:, n + 1:n + 2],
                        norm_b[:, n + 1:n + 2])

            attention_stage(nc, psum, ident, neg_half, "attn2", tiles(h[1], TILE), tiles(x1, TILE),
                            TOK // WIDE, 16, 32, w_q2, w_k2, w_v2, bias2, None, None, 1 / 4,
                            [(w_o2, out_bias2, norm_cols(0)), (w_o2s, out_bias2s[:, :], norm_cols(2))],
                            False)
            kept = [(D // (n + 1), w_dn2s[n]) for n in range(3)]
            mlp_stage(nc, psum, ident, neg_half, "mlp", tiles(h[1], MT), tiles(x1, MT),
                      tiles(h[2], MT), TOK // MW, w_up2, b_up2,
                      [([(D, w_dn2)], b_dn2, norm_cols(4)), (kept, b_dn2s[:, :], norm_cols(6))])

        w_gu = Split(sb, "w_gu", 2 * HID + 2 * EH)
        w_dn_shared, w_dn = sb("w_dn_shared", [P, 6, D]), sb("w_dn", [P, EH // P, D])
        w_dn_mid = sb("w_dn_mid", [P, EXPERTS, D])
        side = MoeWeights(nc, top, sb, w_gu, w_gu_dram, w_dn_shared, ws_down, w_dn, w_down, w_dn_mid)
        attention_stage(nc, psum, ident, neg_half, "attn3", tiles(h[2], TILE), tiles(h[3], TILE),
                        TOK // WIDE, 16, 32, w_q3, w_k3, w_v3, bias3, q_bias3, k_bias3, 1 / 4,
                        [(w_o3, out_bias3, None)], True, side)
        moe_stage(nc, psum, ident, neg_half, "moe", tiles(h[3], MT), tiles(out, MT), TOK // MW, w_gu,
                  w_router, sg_bias[:, :], w_dn_shared, w_dn, w_dn_mid, iota8[:, :])


def kernel(x, L0_tok_W_proj, L0_tok_b_proj, L0_tok_pos_table, L0_attn_W_Q, L0_attn_b_Q, L0_attn_W_K,
           L0_attn_b_K, L0_attn_W_V, L0_attn_b_V, L0_attn_W_O, L0_attn_b_O, L0_ffn_gumbel_weights,
           L0_ffn_n1l_g, L0_ffn_n1l_b, L0_ffn_n1s_g, L0_ffn_n1s_b, L0_ffn_w_qkv, L0_ffn_w_proj,
           L0_ffn_b_proj, L0_ffn_n2l_g, L0_ffn_n2l_b, L0_ffn_n2s_g, L0_ffn_n2s_b, L0_ffn_w_fc1,
           L0_ffn_b_fc1, L0_ffn_w_fc2, L0_ffn_b_fc2, L1_attn_w_qkv, L1_attn_b_qkv, L1_attn_w_proj,
           L1_attn_b_proj, L1_ffn_router_w, L1_ffn_w_gate, L1_ffn_w_up, L1_ffn_w_down, L1_ffn_ws_gate,
           L1_ffn_ws_up, L1_ffn_ws_down, L1_ffn_sg_w, L1_ffn_sg_b):
    import concourse.bacc as _bacc
    from concourse.bass_utils import run_bass_kernel_spmd as _run

    def flat(w):
        return np.asarray(w).transpose(1, 0, 2).reshape(D, -1)

    g = SIDE // PATCH
    patches = np.asarray(x).reshape(IMAGES, g, PATCH, g, PATCH, 3).transpose(2, 4, 5, 0, 1, 3)

    def by_chunk(v):
        return np.asarray(v).reshape(-1, P).T

    def spread(v):
        v = np.asarray(v)
        out = np.zeros((HEADS, 32) + v.shape[1:], v.dtype)
        out[:, 0:16] = v.reshape((HEADS, 16) + v.shape[1:])
        return out.reshape((HEADS * 32 // P, P) + v.shape[1:])

    norms = np.stack([np.asarray(v) for v in (L0_ffn_n1l_g, L0_ffn_n1l_b, L0_ffn_n1s_g, L0_ffn_n1s_b,
                                              L0_ffn_n2l_g, L0_ffn_n2l_b, L0_ffn_n2s_g, L0_ffn_n2s_b)], 1)
    b_qkv3 = np.asarray(L1_attn_b_qkv).reshape(3, D)
    host = {
        "x": patches.reshape(PATCH_K, TOK),
        "tok_w": L0_tok_W_proj, "tok_b": L0_tok_b_proj,
        "pos": np.tile(np.asarray(L0_tok_pos_table), (WIDE // SEQ, 1)).reshape(TILES, TILE, D)
                 .transpose(1, 0, 2),
        "wq1": flat(L0_attn_W_Q), "wk1": flat(L0_attn_W_K), "wv1": flat(L0_attn_W_V),
        "w_qkv2": L0_ffn_w_qkv, "w_fc1": L0_ffn_w_fc1, "w_fc2": L0_ffn_w_fc2,
        "w_qkv3": np.asarray(L1_attn_w_qkv).T,
        "columns_dram": np.concatenate(
            [norms[0:P], np.concatenate([norms[P:D], np.zeros_like(norms[0:DB])]),
             by_chunk(L0_attn_b_Q), by_chunk(L0_attn_b_K), by_chunk(L0_attn_b_V), by_chunk(L0_ffn_b_fc1)]
            + [spread(v).T for v in b_qkv3], axis=1),
        "vectors_dram": np.concatenate([np.asarray(v) for v in (
            L0_attn_b_O, L0_ffn_b_proj, L1_attn_b_proj, L0_ffn_b_fc2, L0_ffn_gumbel_weights, L1_ffn_sg_b)]),
        "w_out_dram": np.concatenate([np.asarray(L0_attn_W_O).reshape(HID // P, P, D),
                                      spread(L0_ffn_w_proj), spread(np.asarray(L1_attn_w_proj).T)]),
        "w_gu_dram": np.concatenate([np.asarray(L1_ffn_ws_gate), np.asarray(L1_ffn_ws_up),
                                     flat(L1_ffn_w_gate), flat(L1_ffn_w_up)], axis=1),
        "w_router_dram": np.concatenate([np.asarray(L1_ffn_router_w)] + 2 * [np.asarray(L1_ffn_sg_w)],
                                        axis=1),
        "w_down": np.asarray(L1_ffn_w_down).reshape(EH, D), "ws_down": L1_ffn_ws_down,
    }
    nc = _bacc.Bacc("TRN2", target_bir_lowering=False, num_devices=1)
    arrays, args = {}, {}
    for name, value in host.items():
        a = np.ascontiguousarray(value)
        arrays["in_" + name] = a
        args[name] = nc.dram_tensor("in_" + name, a.shape, mybir.dt.from_np(a.dtype),
                                    kind="ExternalInput").ap()
    args["out"] = nc.dram_tensor("y", [TOK, D], F32, kind="ExternalOutput").ap()
    build(nc, **args)
    r = _run(nc, [arrays], core_ids=[0])
    return r.results[0]["y"].reshape(IMAGES, SEQ, D)
```
